# Optimizing a Trainium2 kernel written in Bass

```python
import numpy as np
import jax
import jax.numpy as jnp

def _softmax(x, axis=-1):
    return jax.nn.softmax(x, axis=axis)

def _gelu(x):
    return jax.nn.gelu(x, approximate=True)

def _silu(x):
    return jax.nn.silu(x)

def _sigmoid(x):
    return jax.nn.sigmoid(x)

def _layernorm(x, axis=-1, eps=1e-05):
    m = jnp.mean(x, axis=axis, keepdims=True)
    v = jnp.var(x, axis=axis, keepdims=True)
    return (x - m) / jnp.sqrt(v + eps)

def _scatter_add(tgt, idx, src, axis=0):
    return tgt.at[idx].add(src)

def _segment_sum(src, seg, n):
    return jax.ops.segment_sum(src, seg, n)
kernel_name = 'mk_dlrm_tower_d1_rec_r8_4ea075'

def setup_inputs(seed: int=0):
    np.random.seed(seed)
    _w = jnp.asarray

    def _rec_inputs():
        import jax
        import jax.numpy as jnp
        _tk = jax.random.key(seed)
        dense_ctx = jax.random.normal(jax.random.fold_in(_tk, 190), (1024, 16), jnp.float32)
        ids = jnp.stack([jax.random.randint(jax.random.fold_in(_tk, 200 + f), (1024,), 0, v, jnp.int32) for f, v in enumerate([1000, 1000, 1000, 12500, 1000, 1250, 1250, 1000, 12500, 12500, 1250, 1000, 12500, 12500, 1250, 12500, 12500, 125000, 1250, 125000, 125000, 12500, 1000, 12500, 125000, 12500])], axis=1)
        tbl_0 = 0.05 * jax.random.normal(jax.random.fold_in(_tk, 500 + 0), (1000, 32), jnp.float32)
        tbl_1 = 0.05 * jax.random.normal(jax.random.fold_in(_tk, 500 + 1), (1000, 32), jnp.float32)
        tbl_2 = 0.05 * jax.random.normal(jax.random.fold_in(_tk, 500 + 2), (1000, 32), jnp.float32)
        tbl_3 = 0.05 * jax.random.normal(jax.random.fold_in(_tk, 500 + 3), (12500, 32), jnp.float32)
        tbl_4 = 0.05 * jax.random.normal(jax.random.fold_in(_tk, 500 + 4), (1000, 32), jnp.float32)
        tbl_5 = 0.05 * jax.random.normal(jax.random.fold_in(_tk, 500 + 5), (1250, 32), jnp.float32)
        tbl_6 = 0.05 * jax.random.normal(jax.random.fold_in(_tk, 500 + 6), (1250, 32), jnp.float32)
        tbl_7 = 0.05 * jax.random.normal(jax.random.fold_in(_tk, 500 + 7), (1000, 32), jnp.float32)
        tbl_8 = 0.05 * jax.random.normal(jax.random.fold_in(_tk, 500 + 8), (12500, 32), jnp.float32)
        tbl_9 = 0.05 * jax.random.normal(jax.random.fold_in(_tk, 500 + 9), (12500, 32), jnp.float32)
        tbl_10 = 0.05 * jax.random.normal(jax.random.fold_in(_tk, 500 + 10), (1250, 32), jnp.float32)
        tbl_11 = 0.05 * jax.random.normal(jax.random.fold_in(_tk, 500 + 11), (1000, 32), jnp.float32)
        tbl_12 = 0.05 * jax.random.normal(jax.random.fold_in(_tk, 500 + 12), (12500, 32), jnp.float32)
        tbl_13 = 0.05 * jax.random.normal(jax.random.fold_in(_tk, 500 + 13), (12500, 32), jnp.float32)
        tbl_14 = 0.05 * jax.random.normal(jax.random.fold_in(_tk, 500 + 14), (1250, 32), jnp.float32)
        tbl_15 = 0.05 * jax.random.normal(jax.random.fold_in(_tk, 500 + 15), (12500, 32), jnp.float32)
        tbl_16 = 0.05 * jax.random.normal(jax.random.fold_in(_tk, 500 + 16), (12500, 32), jnp.float32)
        tbl_17 = 0.05 * jax.random.normal(jax.random.fold_in(_tk, 500 + 17), (125000, 32), jnp.float32)
        tbl_18 = 0.05 * jax.random.normal(jax.random.fold_in(_tk, 500 + 18), (1250, 32), jnp.float32)
        tbl_19 = 0.05 * jax.random.normal(jax.random.fold_in(_tk, 500 + 19), (125000, 32), jnp.float32)
        tbl_20 = 0.05 * jax.random.normal(jax.random.fold_in(_tk, 500 + 20), (125000, 32), jnp.float32)
        tbl_21 = 0.05 * jax.random.normal(jax.random.fold_in(_tk, 500 + 21), (12500, 32), jnp.float32)
        tbl_22 = 0.05 * jax.random.normal(jax.random.fold_in(_tk, 500 + 22), (1000, 32), jnp.float32)
        tbl_23 = 0.05 * jax.random.normal(jax.random.fold_in(_tk, 500 + 23), (12500, 32), jnp.float32)
        tbl_24 = 0.05 * jax.random.normal(jax.random.fold_in(_tk, 500 + 24), (125000, 32), jnp.float32)
        tbl_25 = 0.05 * jax.random.normal(jax.random.fold_in(_tk, 500 + 25), (12500, 32), jnp.float32)
        _rk = jax.random.fold_in(_tk, 7)
        W_top1 = 0.0606339 * jax.random.normal(jax.random.fold_in(_tk, 801), (272, 512), jnp.float32)
        W_top2 = 0.0441942 * jax.random.normal(jax.random.fold_in(_tk, 802), (512, 256), jnp.float32)
        W_top3 = 0.0625 * jax.random.normal(jax.random.fold_in(_tk, 803), (256, 1), jnp.float32)
        b_top1 = jnp.zeros((512,), jnp.float32)
        b_top2 = jnp.zeros((256,), jnp.float32)
        return (dense_ctx, ids, tbl_0, tbl_1, tbl_2, tbl_3, tbl_4, tbl_5, tbl_6, tbl_7, tbl_8, tbl_9, tbl_10, tbl_11, tbl_12, tbl_13, tbl_14, tbl_15, tbl_16, tbl_17, tbl_18, tbl_19, tbl_20, tbl_21, tbl_22, tbl_23, tbl_24, tbl_25, W_top1, b_top1, W_top2, b_top2, W_top3)
    dense_ctx, ids, tbl_0, tbl_1, tbl_2, tbl_3, tbl_4, tbl_5, tbl_6, tbl_7, tbl_8, tbl_9, tbl_10, tbl_11, tbl_12, tbl_13, tbl_14, tbl_15, tbl_16, tbl_17, tbl_18, tbl_19, tbl_20, tbl_21, tbl_22, tbl_23, tbl_24, tbl_25, W_top1, b_top1, W_top2, b_top2, W_top3 = _rec_inputs()

    def _L0_rec_setup():
        import jax, jax.numpy as jnp
        import numpy as np
        M_FIELDS = 26
        H1 = 128
        H2 = 128
        BATCH = 256
        EMB_K = 32

        def _cin_layer(x_prev, x0, W, b):
            return jnp.einsum('bik,bjk,hij->bhk', x_prev, x0, W) + b[None, :, None]
        key = jax.random.key(seed)
        k0, k1, k2, k3, k4 = jax.random.split(key, 5)
        inputs = jax.random.normal(k0, (BATCH, M_FIELDS, EMB_K), dtype=jnp.float32)
        W1 = jax.random.normal(k1, (H1, M_FIELDS, M_FIELDS), dtype=jnp.float32) * 0.05
        b1 = jax.random.normal(k2, (H1,), dtype=jnp.float32) * 0.05
        W2 = jax.random.normal(k3, (H2, H1, M_FIELDS), dtype=jnp.float32) * 0.05
        b2 = jax.random.normal(k4, (H2,), dtype=jnp.float32) * 0.05
        return {'inputs': inputs, 'W1': W1, 'b1': b1, 'W2': W2, 'b2': b2}
    _L0_rec_all = _L0_rec_setup()
    _L0_rec_in = {k: v for k, v in _L0_rec_all.items() if k in ('W1', 'b1', 'W2', 'b2')}
    del _L0_rec_all
    return {'dense_ctx': dense_ctx, 'ids': ids, 'tbl_0': tbl_0, 'tbl_1': tbl_1, 'tbl_2': tbl_2, 'tbl_3': tbl_3, 'tbl_4': tbl_4, 'tbl_5': tbl_5, 'tbl_6': tbl_6, 'tbl_7': tbl_7, 'tbl_8': tbl_8, 'tbl_9': tbl_9, 'tbl_10': tbl_10, 'tbl_11': tbl_11, 'tbl_12': tbl_12, 'tbl_13': tbl_13, 'tbl_14': tbl_14, 'tbl_15': tbl_15, 'tbl_16': tbl_16, 'tbl_17': tbl_17, 'tbl_18': tbl_18, 'tbl_19': tbl_19, 'tbl_20': tbl_20, 'tbl_21': tbl_21, 'tbl_22': tbl_22, 'tbl_23': tbl_23, 'tbl_24': tbl_24, 'tbl_25': tbl_25, 'W_top1': W_top1, 'b_top1': b_top1, 'W_top2': W_top2, 'b_top2': b_top2, 'W_top3': W_top3, 'L0_rec_W1': _L0_rec_in['W1'], 'L0_rec_b1': _L0_rec_in['b1'], 'L0_rec_W2': _L0_rec_in['W2'], 'L0_rec_b2': _L0_rec_in['b2']}

def reference(dense_ctx, ids, tbl_0, tbl_1, tbl_2, tbl_3, tbl_4, tbl_5, tbl_6, tbl_7, tbl_8, tbl_9, tbl_10, tbl_11, tbl_12, tbl_13, tbl_14, tbl_15, tbl_16, tbl_17, tbl_18, tbl_19, tbl_20, tbl_21, tbl_22, tbl_23, tbl_24, tbl_25, W_top1, b_top1, W_top2, b_top2, W_top3, L0_rec_W1, L0_rec_b1, L0_rec_W2, L0_rec_b2):
    import jax
    import jax.numpy as jnp

    def _L0_rec_ref(inputs, W1, b1, W2, b2):
        import jax, jax.numpy as jnp
        import numpy as np
        M_FIELDS = 26
        H1 = 128
        H2 = 128
        BATCH = 256
        EMB_K = 32

        def _cin_layer(x_prev, x0, W, b):
            return jnp.einsum('bik,bjk,hij->bhk', x_prev, x0, W) + b[None, :, None]
        x1 = _cin_layer(inputs, inputs, W1, b1)
        x2 = _cin_layer(x1, inputs, W2, b2)
        res = jnp.concatenate([x1, x2], axis=1)
        return jnp.sum(res, axis=-1)
    e = jnp.stack([tbl_0[ids[:, 0]], tbl_1[ids[:, 1]], tbl_2[ids[:, 2]], tbl_3[ids[:, 3]], tbl_4[ids[:, 4]], tbl_5[ids[:, 5]], tbl_6[ids[:, 6]], tbl_7[ids[:, 7]], tbl_8[ids[:, 8]], tbl_9[ids[:, 9]], tbl_10[ids[:, 10]], tbl_11[ids[:, 11]], tbl_12[ids[:, 12]], tbl_13[ids[:, 13]], tbl_14[ids[:, 14]], tbl_15[ids[:, 15]], tbl_16[ids[:, 16]], tbl_17[ids[:, 17]], tbl_18[ids[:, 18]], tbl_19[ids[:, 19]], tbl_20[ids[:, 20]], tbl_21[ids[:, 21]], tbl_22[ids[:, 22]], tbl_23[ids[:, 23]], tbl_24[ids[:, 24]], tbl_25[ids[:, 25]]], axis=1)
    z = _L0_rec_ref(e, L0_rec_W1, L0_rec_b1, L0_rec_W2, L0_rec_b2)
    z = z.reshape(z.shape[0], -1)
    h = jnp.concatenate([z, dense_ctx], axis=1)
    h = jnp.maximum(h @ W_top1 + b_top1, 0.0)
    h = jnp.maximum(h @ W_top2 + b_top2, 0.0)
    y = h @ W_top3
    return y

_drawn_inputs = setup_inputs


def setup_inputs(seed=0):
    import zlib

    import numpy as np

    out = dict(_drawn_inputs(seed))
    spreads = {'b_top1': (0.0, 2.0), 'b_top2': (0.0, 0.8)}
    factors = {'tbl_0': 8.0,
     'tbl_1': 8.0,
     'tbl_2': 8.0,
     'tbl_3': 8.0,
     'tbl_4': 8.0,
     'tbl_5': 8.0,
     'tbl_6': 8.0,
     'tbl_7': 8.0,
     'tbl_8': 8.0,
     'tbl_9': 8.0,
     'tbl_10': 8.0,
     'tbl_11': 8.0,
     'tbl_12': 8.0,
     'tbl_13': 8.0,
     'tbl_14': 8.0,
     'tbl_15': 8.0,
     'tbl_16': 8.0,
     'tbl_17': 8.0,
     'tbl_18': 8.0,
     'tbl_19': 8.0,
     'tbl_20': 8.0,
     'tbl_21': 7.832,
     'tbl_22': 8.0,
     'tbl_23': 8.0,
     'tbl_24': 8.0,
     'tbl_25': 8.0,
     'L0_rec_W1': 8.0,
     'L0_rec_W2': 4.122,
     'dense_ctx': 5.8}
    for name, (base, spread) in spreads.items():
        noise = np.random.default_rng([zlib.crc32(name.encode()), seed]).standard_normal(out[name].shape)
        drawn = base * np.exp(spread * noise) if base else spread * noise
        out[name] = jnp.asarray(drawn.astype(out[name].dtype))
    for name, factor in factors.items():
        out[name] = (out[name] * factor).astype(out[name].dtype)
    return out
```

```python
from contextlib import ExitStack

import concourse.bass as bass
from concourse import mybir

F32 = mybir.dt.float32
I32 = mybir.dt.int32
U32 = mybir.dt.uint32
ALU = mybir.AluOpType
ACT = mybir.ActivationFunctionType

P = 128
NF = 26
K = 32
NJ = NF + 1
NG = P // K
NS = P // NG
SETS = (15, 6, 5)
FIRST = (0, 15, 21)
NA, NB, NC = SETS
NX = NB + NC

AA0 = 0
ONE = 120
BB0 = 121
AX0 = 142
BC0 = AX0 + NX * NA
CC0 = BC0 + NC * NB
NP = CC0 + 3 * NC
AC0 = AX0 + NB * NA
ROW0 = (0, BB0, AC0)
ROWS = (BB0, AC0 - BB0, NP - AC0)
assert NP == 352 and max(ROWS) <= P

WRAP = (7, 2, 2)
XE0 = (0, 22, 30)
XE = 37

VT0 = (0, 27, 39)
NVT = 45
JS = tuple(NJ - f for f in FIRST)
T0 = (0, JS[0] * P, (JS[0] + JS[1]) * P)
TLEN = sum(JS) * P

PER = (4, 8, 16)
FILLS = tuple(NS // n for n in PER)
FILL0 = (0, 8, 12)
NFILL = sum(FILLS)
RING = 4

W2_FILL0, W2_FILLS = 0, 7
DN_FILL0, DN_FILLS = 7, 2
V_FILL0, V_FILLS = 9, NF
VT_FILL0 = V_FILL0 + V_FILLS
VT_BLOCKS = [(x, j, min(4, JS[x] - j)) for x in range(3) for j in range(0, JS[x], 4)]
PRE = VT_FILL0 + len(VT_BLOCKS)
BY_VECTOR = [n for n in range(PRE) if (n < DN_FILL0 and n % 2) or (n >= VT_FILL0 and n % 2)]


def emptied_by_vector(n):
    return len([f for f in BY_VECTOR if f <= n])


def emptied_by_scalar(n):
    return n + 1 - emptied_by_vector(n)


def shifts(n, full):
    runs = [(0, 0, 0, n)]
    for d in range(1, full):
        runs += [(d, 0, d, n - d), (d, n - d, 0, d)]
    if n % 2 == 0:
        runs.append((full, 0, full, n // 2))
    return runs


def dlrm_kernel(nc, dense, ids, tables, wt1, bt1, wt2, bt2, wt3, w1, b1, w2, b2, out):
    BATCH, DD = dense.shape
    NT = BATCH // P
    H1, H2 = wt1.shape[1], wt2.shape[1]
    C1, C2 = H1 // P, H2 // P
    assert NT % 2 == 0 and NT >= 4

    with ExitStack() as ctx:
        def sb(name, shape, dt=F32):
            return ctx.enter_context(nc.sbuf_tensor(name, shape, dt))

        def psum(name):
            return ctx.enter_context(nc.psum_tensor(name, [P, 512], F32))

        def sem(name):
            return ctx.enter_context(nc.semaphore(name))

        ids_sb = sb("ids_sb", [P, NT, NF], I32)
        ids_now = [sb(f"ids_now{i}", [P, NF], I32) for i in range(2)]
        emb = [sb(f"emb{i}", [P, NF * K]) for i in range(2)]
        xe = sb("xe", [P, XE * NS])
        pairs = sb("pairs", [P, NS, NP])
        bd = [sb(f"bd{i}", [P, NS, NG, NJ]) for i in range(2)]
        shared = sb("shared", [P, NF * NP])
        v = shared
        prod = shared
        w2_sb = shared[:, NF * NP - P * NF:NF * NP].rearrange("h (i j) -> h i j", j=NF)
        w2t = sb("w2t", [P, NF, P])
        w1_sb = sb("w1_sb", [P, NF * NF])
        w1s = sb("w1s", [P, NP])
        vt = sb("vt", [P, NVT, P])
        ident = sb("ident", [P, P])
        wt1_sb = sb("wt1_sb", [P, 2, H1])
        wt1d_sb = sb("wt1d_sb", [DD, H1])
        wt2_sb = sb("wt2_sb", [P, C1, H2])
        wt3_sb = sb("wt3_sb", [P, C2])
        bt1_sb = sb("bt1_sb", [P, C1])
        bt2_sb = sb("bt2_sb", [P, C2])
        b2_sb = sb("b2_sb", [P, 1])
        b2k = sb("b2k", [P, 1])
        dense_sb = sb("dense_sb", [P, NT, DD])
        dense_t = sb("dense_t", [DD, BATCH])
        z_sb = sb("z_sb", [P, 2, P])
        h1_sb = sb("h1_sb", [P, C1, P])
        h2_sb = sb("h2_sb", [P, C2, P])
        y_sb = sb("y_sb", [1, BATCH])

        ring = [psum(f"ring{i}") for i in range(RING)]
        z_ps = psum("z_ps")
        h1_ps = psum("h1_ps")
        h2_ps = psum("h2_ps")

        ids_in = sem("ids_in")
        w1_in = sem("w1_in")
        w2_in = sem("w2_in")
        dense_in = sem("dense_in")
        mlp_in = sem("mlp_in")
        zeroed = sem("zeroed")
        ident_ready = sem("ident_ready")
        cleared_vec = sem("cleared_vec")
        ids_copied = sem("ids_copied")
        gathered = [[sem(f"gathered{i}{x}") for x in "abc"] for i in range(2)]
        emb_used = [sem(f"emb_used{i}") for i in range(2)]
        w1_folded = sem("w1_folded")
        v_folding = sem("v_folding")
        fills = sem("fills")
        emptied_s = sem("emptied_s")
        emptied_v = sem("emptied_v")
        xe_ready = [sem(f"xe_ready{x}") for x in "abc"]
        pairs_ready = [sem(f"pairs_ready{x}") for x in "abc"]
        bd_ready = sem("bd_ready")
        b2_scaled = sem("b2_scaled")
        z_done, z_ready = sem("z_done"), sem("z_ready")
        h1_done, h1_ready = sem("h1_done"), sem("h1_ready")
        h2_done, h2_ready = sem("h2_done"), sem("h2_ready")
        y_done, y_ready = sem("y_done"), sem("y_ready")
        out_done = sem("out_done")

        def view(tensor, offset, dims, part=P):
            base = tensor[:]
            return bass.AP(tensor=base.tensor, offset=base.offset + offset,
                           ap=[[base.ap[0][0], part]] + [[s, c] for s, c in dims])

        def ring_of(n):
            return ring[n % RING]

        block = ctx.enter_context(nc.Block())

        @block.sync
        def _(sp):
            sp.dma_start(ids_sb[:], ids.rearrange("(t p) f -> p t f", p=P)).then_inc(ids_in, 16)
            sp.dma_start(w2_sb, w2).then_inc(w2_in, 16)
            sp.dma_start(w1_sb[:], w1.rearrange("i p q -> i (p q)")).then_inc(w1_in, 16)
            with nc.allow_non_contiguous_dma(reason="one value per partition"):
                sp.dma_start(w1s[:, ONE:ONE + 1], b1.rearrange("(i o) -> i o", o=1)).then_inc(w1_in, 16)
            sp.dma_start(dense_sb[:], dense.rearrange("(t p) d -> p t d", p=P)).then_inc(dense_in, 16)
            sp.dma_start(wt1_sb[:], wt1[0:2 * P, :].rearrange("(c p) n -> p c n", p=P)).then_inc(mlp_in, 16)
            sp.dma_start(wt1d_sb[:], wt1[2 * P:2 * P + DD, :]).then_inc(mlp_in, 16)
            sp.dma_start(wt2_sb[:], wt2.rearrange("(c p) n -> p c n", p=P)).then_inc(mlp_in, 16)
            with nc.allow_non_contiguous_dma(reason="one value per partition"):
                sp.dma_start(wt3_sb[:], wt3.rearrange("(c p) o -> p (c o)", p=P)).then_inc(mlp_in, 16)
                sp.dma_start(bt1_sb[:], bt1.rearrange("(c p) -> p c", p=P)).then_inc(mlp_in, 16)
                sp.dma_start(bt2_sb[:], bt2.rearrange("(c p) -> p c", p=P)).then_inc(mlp_in, 16)
                sp.dma_start(b2_sb[:], b2.rearrange("(h o) -> h o", o=1)).then_inc(mlp_in, 16)
            sp.wait_ge(y_ready, NT)
            sp.dma_start(out.rearrange("b o -> o b"), y_sb[:]).then_inc(out_done, 16)
            sp.wait_ge(out_done, 16)

        @block.gpsimd
        def _(pool):
            nc.gpsimd.memset(ident[:], 0.0)
            nc.gpsimd.memset(bd[0][:], 0.0).then_inc(zeroed, 1)
            pool.wait_ge(zeroed, 1)
            nc.gpsimd.affine_select(out=ident[:], in_=ident[:], compare_op=ALU.not_equal, fill=1.0,
                                    base=0, pattern=[[-1, P]], channel_multiplier=1).then_inc(ident_ready, 1)
            pool.wait_ge(ids_in, 16)
            with pool.Fori(0, NT // 2) as i:
                for par in range(2):
                    pool.wait_ge(emb_used[par], i + 1)
                    nc.gpsimd.tensor_copy(ids_now[par][:], ids_sb[:, bass.ds(i * 2 + par, 1), :]
                                          ).then_inc(ids_copied, 1)
                    pool.wait_ge(ids_copied, i * 2 + par + 1)
                    pool.nop(nofuse=True)
                    for x in range(3):
                        for f in range(FIRST[x], FIRST[x] + SETS[x]):
                            pool.indirect_dma_start(
                                out=emb[par][:, K * f:K * f + K], out_offset=None, in_=tables[f][:, :],
                                in_offset=bass.IndirectOffsetOnAxis(
                                    ap=ids_now[par][:, f:f + 1].bitcast(U32), axis=0),
                            ).then_inc(gathered[par][x], 16)

        @block.vector
        def _(dve):
            nc.vector.memset(bd[1][:], 0.0).then_inc(cleared_vec, 1)
            nc.vector.memset(pairs[:, :, ONE:ONE + 1], 1.0)
            dve.wait_ge(cleared_vec, 1)
            dve.wait_ge(zeroed, 1)
            for par in range(2):
                for g in range(NG - 1):
                    nc.vector.memset(bd[par][K * g:K * g + K, :, g, NF], 1.0)
                nc.vector.memset(bd[par][K * (NG - 1):P, :, NG - 1, NF], 1.0).then_inc(emb_used[par], 1)

            dve.wait_ge(w1_in, 32)
            for n, f0, full, c0 in ((NA, 0, 8, AA0), (NB, FIRST[1], 3, BB0), (NC, FIRST[2], 3, CC0)):
                for d, p, q, m in shifts(n, full):
                    dst = view(w1s, c0 + d * n + p, [(1, m)])
                    pq = view(w1_sb, (f0 + p) * NF + f0 + q, [(NF + 1, m)])
                    qp = view(w1_sb, (f0 + q) * NF + f0 + p, [(NF + 1, m)])
                    if d == 0:
                        nc.vector.tensor_copy(dst, pq)
                    else:
                        nc.vector.tensor_tensor(dst, pq, qp, ALU.add)
            nc.vector.tensor_tensor(view(w1s, AX0, [(NA, NX), (1, NA)]),
                                    view(w1_sb, FIRST[1], [(1, NX), (NF, NA)]),
                                    view(w1_sb, FIRST[1] * NF, [(NF, NX), (1, NA)]), ALU.add)
            nc.vector.tensor_tensor(view(w1s, BC0, [(NB, NC), (1, NB)]),
                                    view(w1_sb, FIRST[1] * NF + FIRST[2], [(1, NC), (NF, NB)]),
                                    view(w1_sb, FIRST[2] * NF + FIRST[1], [(NF, NC), (1, NB)]),
                                    ALU.add).then_inc(w1_folded, 1)

            for n in range(1, W2_FILLS, 2):
                dve.wait_ge(fills, n + 1)
                m = min(4, NF - 4 * n)
                nc.vector.tensor_copy(w2t[:, 4 * n:4 * n + m, :].rearrange("i j h -> i (j h)"),
                                      ring_of(n)[:, 0:m * P]).then_inc(emptied_v, 1)

            def transpose_set(x, t, par):
                dve.wait_ge(gathered[par][x], (t + (2 - par)) * (8 * SETS[x]))
                if x == 0:
                    dve.wait_ge(bd_ready, t)
                    dve.wait_ge(pairs_ready[2], t)
                src = emb[par][:, K * FIRST[x]:K * (FIRST[x] + SETS[x])]
                nc.vector.transpose(xe[:, XE0[x] * NS:(XE0[x] + SETS[x]) * NS], src)
                w0 = XE0[x] + SETS[x]
                last = nc.vector.transpose(xe[:, w0 * NS:(w0 + WRAP[x]) * NS], src[:, 0:K * WRAP[x]])
                last.then_inc(xe_ready[x], 1)
                dve.wait_ge(xe_ready[x], t + 1)

            def cross(col, n_out, f_out, n_in, f_in):
                return nc.vector.tensor_tensor(
                    view(pairs, col, [(NP, NS), (n_in, n_out), (1, n_in)]),
                    view(xe, f_out * NS, [(1, NS), (NS, n_out), (0, n_in)]),
                    view(xe, f_in * NS, [(1, NS), (0, n_out), (NS, n_in)]), ALU.mult)

            def within(col, n, f, d0, nd, m):
                return nc.vector.tensor_tensor(
                    view(pairs, col, [(NP, NS), (n, nd), (1, m)]),
                    view(xe, f * NS, [(1, NS), (0, nd), (NS, m)]),
                    view(xe, (f + d0) * NS, [(1, NS), (NS, nd), (NS, m)]), ALU.mult)

            def free_pairs(x, t):
                if isinstance(t, int) and t == 0:
                    return
                dve.wait_ge(fills, t * NFILL + (PRE - NFILL + FILL0[x] + FILLS[x]))

            def pairs_a(t, par):
                transpose_set(0, t, par)
                free_pairs(0, t)
                within(AA0, NA, XE0[0], 0, 8, NA).then_inc(pairs_ready[0], 1)

            def pairs_bc(t, par):
                transpose_set(1, t, par)
                free_pairs(1, t)
                within(BB0, NB, XE0[1], 0, 3, NB)
                within(BB0 + 3 * NB, NB, XE0[1], 3, 1, 3)
                cross(AX0, NB, XE0[1], NA, XE0[0]).then_inc(pairs_ready[1], 1)
                transpose_set(2, t, par)
                free_pairs(2, t)
                cross(AC0, NC, XE0[2], NA, XE0[0]).then_inc(emb_used[par], 1)
                cross(BC0, NC, XE0[2], NB, XE0[1])
                within(CC0, NC, XE0[2], 0, 3, NC).then_inc(pairs_ready[2], 1)

            def fold(dst_j, dst_col, dst_dims, src_j, src_col, src_dims):
                dst = view(v, dst_j * NP + dst_col, dst_dims)
                return nc.vector.tensor_tensor(dst, dst, view(v, src_j * NP + src_col, src_dims), ALU.add)

            def fold_v():
                B0, C0 = FIRST[1], FIRST[2]
                dve.wait_ge(emptied_s, emptied_by_scalar(V_FILL0 + V_FILLS - 1))
                for half in range(2):
                    if half:
                        dve.wait_ge(v_folding, 1)
                    for d, p, q, m in shifts(NA, 8):
                        if half and d == 0:
                            continue
                        j, a = ((p, q), (q, p))[half]
                        last = fold(B0, d * NA + p, [(NP, NX), (1, m)], j, AX0 + a, [(NA, NX), (NP + 1, m)])
                    for d, p, q, m in shifts(NB, 3):
                        if half and d == 0:
                            continue
                        j, b = ((p, q), (q, p))[half]
                        last = fold(C0, BB0 + d * NB + p, [(NP, NC), (1, m)],
                                    B0 + j, BC0 + b, [(NB, NC), (NP + 1, m)])
                    dst = [(NP, NC), (NA, NB), (1, NA)]
                    if half:
                        last = fold(C0, AX0, dst, 0, BC0, [(NB, NC), (1, NB), (NP, NA)])
                    else:
                        last = fold(C0, AX0, dst, B0, AC0, [(NA, NC), (NP, NB), (1, NA)])
                        for d, p, q, m in shifts(NB, 3):
                            last = fold(B0 + q, AX0 + p * NA, [(NP + NA, m), (1, NA)],
                                        0, BB0 + d * NB + p, [(1, m), (NP, NA)])
                        for d, p, q, m in shifts(NC, 3):
                            last = fold(C0 + q, AC0 + p * NA, [(NP + NA, m), (1, NA)],
                                        0, CC0 + d * NC + p, [(1, m), (NP, NA)])
                            last = fold(C0 + q, BC0 + p * NB, [(NP + NB, m), (1, NB)],
                                        B0, CC0 + d * NC + p, [(1, m), (NP, NB)])
                    last.then_inc(v_folding, 1)

            pairs_a(0, 0)
            fold_v()
            for n in [f for f in BY_VECTOR if f >= VT_FILL0]:
                x, j, m = VT_BLOCKS[n - VT_FILL0]
                dve.wait_ge(fills, n + 1)
                nc.vector.tensor_copy(
                    vt[0:ROWS[x], VT0[x] + j:VT0[x] + j + m, :].rearrange("r j h -> r (j h)"),
                    ring_of(n)[0:ROWS[x], 0:m * P]).then_inc(emptied_v, 1)
            pairs_bc(0, 0)
            with dve.Fori(0, NT // 2 - 1) as i:
                for u in range(2):
                    pairs_a(i * 2 + 1 + u, 1 - u)
                    pairs_bc(i * 2 + 1 + u, 1 - u)
            pairs_a(NT - 1, 1)
            pairs_bc(NT - 1, 1)

        @block.scalar
        def _(act):
            def copy(dst, src):
                return nc.scalar.activation(dst, src, ACT.Copy)

            def fill_block_diagonal(x, t, par):
                act.wait_ge(xe_ready[x], t + 1)
                for g in range(NG):
                    rows = slice(K * g, K * g + K)
                    last = copy(bd[par][rows, :, g, FIRST[x]:FIRST[x] + SETS[x]],
                                xe[rows, XE0[x] * NS:(XE0[x] + SETS[x]) * NS].rearrange(
                                    "p (f s) -> p s f", s=NS))
                if x == 2:
                    last.then_inc(bd_ready, 1)

            def empty_products(x, t, par):
                for m in range(FILLS[x]):
                    act.wait_ge(fills, t * NFILL + (PRE + FILL0[x] + m + 1))
                    src = ring_of(PRE + par * NFILL + FILL0[x] + m)[0:ROWS[x], 0:PER[x] * NG * JS[x]]
                    dst = prod[0:ROWS[x], T0[x]:T0[x] + JS[x] * P].rearrange(
                        "r (j g s) -> r s g j", g=NG, s=NS)[:, m * PER[x]:(m + 1) * PER[x]]
                    copy(dst, src.rearrange("r (u g j) -> r u g j", g=NG, j=JS[x])).then_inc(emptied_s, 1)

            def empty_h1(t):
                act.wait_ge(h1_done, t + 1)
                for c in range(C1):
                    last = nc.scalar.activation(h1_sb[:, c, :], h1_ps[:, P * c:P * c + P], ACT.Relu,
                                                bias=bt1_sb[:, c:c + 1])
                last.then_inc(h1_ready, 1)

            def empty_h2(t):
                act.wait_ge(h2_done, t + 1)
                for c in range(C2):
                    last = nc.scalar.activation(h2_sb[:, c, :], h2_ps[:, P * c:P * c + P], ACT.Relu,
                                                bias=bt2_sb[:, c:c + 1])
                last.then_inc(h2_ready, 1)

            def empty_y(t):
                act.wait_ge(y_done, t + 1)
                copy(y_sb[:, bass.ds(t * P, P)], h2_ps[0:1, C2 * P:C2 * P + P]).then_inc(y_ready, 1)

            def empty_z(t):
                act.wait_ge(z_done, t + 1)
                copy(z_sb[:, 0, :], z_ps[:, P:2 * P])
                nc.scalar.activation(z_sb[:, 1, :], z_ps[:, 0:P], ACT.Identity,
                                     bias=b2k[:, 0:1]).then_inc(z_ready, 1)

            def tile(t, par, first=False, last=False):
                empty_products(0, t, par)
                if not first:
                    empty_h1(t - 1)
                empty_products(1, t, par)
                if not first:
                    empty_h2(t - 1)
                empty_products(2, t, par)
                if not first:
                    empty_y(t - 1)
                if not last:
                    fill_block_diagonal(0, t + 1, 1 - par)
                    fill_block_diagonal(1, t + 1, 1 - par)
                empty_z(t)
                if not last:
                    fill_block_diagonal(2, t + 1, 1 - par)

            for n in range(0, W2_FILLS, 2):
                act.wait_ge(fills, n + 1)
                m = min(4, NF - 4 * n)
                copy(w2t[:, 4 * n:4 * n + m, :].rearrange("i j h -> i (j h)"),
                     ring_of(n)[:, 0:m * P]).then_inc(emptied_s, 1)
            for n in range(DN_FILLS):
                act.wait_ge(fills, DN_FILL0 + n + 1)
                copy(dense_t[:, 4 * P * n:4 * P * n + 4 * P], ring_of(DN_FILL0 + n)[0:DD, :]
                     ).then_inc(emptied_s, 1)
            for j in range(NF):
                act.wait_ge(fills, V_FILL0 + j + 1)
                copy(v[:, j * NP:j * NP + NP], ring_of(V_FILL0 + j)[:, 0:NP]).then_inc(emptied_s, 1)
            act.wait_ge(mlp_in, 7 * 16)
            nc.scalar.mul(b2k[:], b2_sb[:], float(K)).then_inc(b2_scaled, 1)
            act.wait_ge(emb_used[0], 1)
            act.wait_ge(emb_used[1], 1)
            fill_block_diagonal(0, 0, 0)
            for n in range(VT_FILL0, PRE):
                if n in BY_VECTOR:
                    continue
                x, j, m = VT_BLOCKS[n - VT_FILL0]
                act.wait_ge(fills, n + 1)
                copy(vt[0:ROWS[x], VT0[x] + j:VT0[x] + j + m, :].rearrange("r j h -> r (j h)"),
                     ring_of(n)[0:ROWS[x], 0:m * P]).then_inc(emptied_s, 1)
            fill_block_diagonal(1, 0, 0)
            fill_block_diagonal(2, 0, 0)
            act.wait_ge(b2_scaled, 1)
            tile(0, 0, first=True)
            with act.Fori(0, NT // 2 - 1) as i:
                for u in range(2):
                    tile(i * 2 + 1 + u, 1 - u)
            tile(NT - 1, 1, last=True)
            empty_h1(NT - 1)
            empty_h2(NT - 1)
            empty_y(NT - 1)

        @block.tensor
        def _(pe):
            def early_slot(n):
                if n >= RING:
                    if n - RING in BY_VECTOR:
                        pe.wait_ge(emptied_v, emptied_by_vector(n - RING))
                    else:
                        pe.wait_ge(emptied_s, emptied_by_scalar(n - RING))

            def products(x, t, par, first):
                pe.wait_ge(pairs_ready[x], t + 1)
                if x == 0:
                    pe.wait_ge(bd_ready, t + 1)
                n = NG * JS[x]
                for m in range(FILLS[x]):
                    if not first or FILL0[x] + m >= RING:
                        pe.wait_ge(emptied_s, t * NFILL + (emptied_by_scalar(PRE - 1) + FILL0[x] + m - RING + 1))
                    for u in range(PER[x]):
                        s = m * PER[x] + u
                        mm = pe.matmul(ring_of(PRE + par * NFILL + FILL0[x] + m)[0:ROWS[x], u * n:u * n + n],
                                       pairs[:, s, ROW0[x]:ROW0[x] + ROWS[x]],
                                       bd[par][:, s, :, FIRST[x]:NJ], start=True, stop=True)
                    mm.then_inc(fills, 1)

            def interactions(t):
                pe.wait_ge(emptied_s, t * NFILL + (emptied_by_scalar(PRE - 1) + NFILL))
                z2_terms = [(x, j) for x in range(3) for j in range(JS[x] - 1)]
                z1_terms = [(x, JS[x] - 1) for x in range(3)]
                for dst, blocks in ((z_ps[:, 0:P], z2_terms), (z_ps[:, P:2 * P], z1_terms)):
                    for x, j in blocks:
                        mm = pe.matmul(dst, vt[0:ROWS[x], VT0[x] + j, :],
                                       prod[0:ROWS[x], T0[x] + j * P:T0[x] + j * P + P],
                                       start=(x, j) == blocks[0], stop=(x, j) == blocks[-1])
                mm.then_inc(z_done, 1)

            def layer1(t):
                pe.wait_ge(z_ready, t + 1)
                for c in range(C1):
                    cols = slice(P * c, P * c + P)
                    pe.matmul(h1_ps[:, cols], wt1_sb[:, 0, cols], z_sb[:, 0, :], start=True, stop=False)
                    pe.matmul(h1_ps[:, cols], wt1_sb[:, 1, cols], z_sb[:, 1, :], start=False, stop=False)
                    mm = pe.matmul(h1_ps[:, cols], wt1d_sb[:, cols], dense_t[:, bass.ds(t * P, P)],
                                   start=False, stop=True)
                mm.then_inc(h1_done, 1)

            def layer2(t):
                pe.wait_ge(h1_ready, t + 1)
                for c in range(C2):
                    for k in range(C1):
                        mm = pe.matmul(h2_ps[:, P * c:P * c + P], wt2_sb[:, k, P * c:P * c + P],
                                       h1_sb[:, k, :], start=(k == 0), stop=(k == C1 - 1))
                mm.then_inc(h2_done, 1)

            def layer3(t):
                pe.wait_ge(h2_ready, t + 1)
                for k in range(C2):
                    mm = pe.matmul(h2_ps[0:1, C2 * P:C2 * P + P], wt3_sb[:, k:k + 1], h2_sb[:, k, :],
                                   start=(k == 0), stop=(k == C2 - 1))
                mm.then_inc(y_done, 1)

            def tile(t, par, first=False):
                products(0, t, par, first)
                if not first:
                    layer1(t - 1)
                products(1, t, par, first)
                if not first:
                    layer2(t - 1)
                products(2, t, par, first)
                if not first:
                    layer3(t - 1)
                interactions(t)

            pe.wait_ge(ident_ready, 1)
            pe.wait_ge(w2_in, 16)
            for n in range(W2_FILLS):
                early_slot(n)
                for u in range(min(4, NF - 4 * n)):
                    mm = pe.transpose(ring_of(n)[:, P * u:P * u + P], w2_sb[:, :, 4 * n + u], ident[:])
                mm.then_inc(fills, 1)
            pe.wait_ge(dense_in, 16)
            for n in range(DN_FILLS):
                early_slot(DN_FILL0 + n)
                for u in range(4):
                    mm = pe.transpose(ring_of(DN_FILL0 + n)[0:DD, P * u:P * u + P],
                                      dense_sb[:, 4 * n + u, :], ident[:])
                mm.then_inc(fills, 1)
            pe.wait_ge(w1_folded, 1)
            pe.wait_ge(emptied_v, emptied_by_vector(W2_FILLS - 1))
            pe.wait_ge(emptied_s, emptied_by_scalar(W2_FILLS - 1))
            for j in range(NF):
                early_slot(V_FILL0 + j)
                pe.matmul(ring_of(V_FILL0 + j)[:, 0:NP], w2t[:, j, :], w1s[:],
                          start=True, stop=True).then_inc(fills, 1)
            pe.wait_ge(v_folding, 2)
            for k, (x, j0, m) in enumerate(VT_BLOCKS):
                early_slot(VT_FILL0 + k)
                for u in range(m):
                    j = FIRST[x] + j0 + u
                    src = w1s if j == NF else v
                    c0 = ROW0[x] if j == NF else j * NP + ROW0[x]
                    mm = pe.transpose(ring_of(VT_FILL0 + k)[0:ROWS[x], P * u:P * u + P],
                                      src[:, c0:c0 + ROWS[x]], ident[:])
                mm.then_inc(fills, 1)
            pe.wait_ge(emptied_v, emptied_by_vector(PRE - 1))
            pe.wait_ge(emptied_s, emptied_by_scalar(PRE - 1))
            pe.wait_ge(mlp_in, 7 * 16)
            tile(0, 0, first=True)
            with pe.Fori(0, NT // 2 - 1) as i:
                for u in range(2):
                    tile(i * 2 + 1 + u, 1 - u)
            tile(NT - 1, 1)
            layer1(NT - 1)
            layer2(NT - 1)
            layer3(NT - 1)


def kernel(**inputs):
    import numpy as np
    import concourse.bacc as bacc
    from concourse.bass_utils import run_bass_kernel_spmd

    nc = bacc.Bacc("TRN2", target_bir_lowering=False, num_devices=1)
    arrays = {}

    def dram(name):
        a = np.ascontiguousarray(inputs[name])
        arrays[f"in_{name}"] = a
        return nc.dram_tensor(f"in_{name}", a.shape, mybir.dt.from_np(a.dtype), kind="ExternalInput").ap()

    tables = [dram(f"tbl_{f}") for f in range(26)]
    dense, ids = dram("dense_ctx"), dram("ids")
    mlp = [dram(n) for n in ("W_top1", "b_top1", "W_top2", "b_top2", "W_top3")]
    cin = [dram(n) for n in ("L0_rec_W1", "L0_rec_b1", "L0_rec_W2", "L0_rec_b2")]
    out = nc.dram_tensor("out_y", (dense.shape[0], 1), F32, kind="ExternalOutput").ap()
    dlrm_kernel(nc, dense, ids, tables, *mlp, *cin, out)
    r = run_bass_kernel_spmd(nc, [arrays], core_ids=[0])
    return r.results[0]["out_y"]
```

```python
from contextlib import ExitStack

import concourse.bass as bass
from concourse import mybir

F32 = mybir.dt.float32
I32 = mybir.dt.int32
U32 = mybir.dt.uint32
ALU = mybir.AluOpType
ACT = mybir.ActivationFunctionType

P = 128
NF = 26
K = 32
NJ = NF + 1
NG = P // K
NS = P // NG
SETS = (14, 12)
FIRST = (0, 14)
NA, NW = SETS


def shifts(n):
    runs = [(0, 0, 0, n)]
    for d in range(1, (n + 1) // 2):
        runs += [(d, 0, d, n - d), (d, n - d, 0, d)]
    if n % 2 == 0:
        runs.append((n // 2, 0, n // 2, n // 2))
    return runs


ONE = 0
ONE_A = 1
AA = ONE_A + NA
WW = AA + NA * (NA + 1) // 2
ROWS = (WW, NW * (NW + 1) // 2)
ROW0 = (0, WW)
NP = sum(ROWS)
AW = NP
NV = NP + NW * NA
assert max(ROWS) <= P and NV <= 512

WRAP = (NA // 2 - 1, NW // 2 - 1)
XE0 = (0, NA + WRAP[0])
XE = XE0[1] + NW + WRAP[1]

CROSS_W = NW // 2
CROSS = CROSS_W * NA
VT0 = (0, NJ)
VT_CROSS = 2 * NJ
NVT = VT_CROSS + 2

PER = 4
FILLS = NS // PER
NFILL = 2 * FILLS
LATE = FILLS + FILLS // 2
RING = 4

W2_FILL0, W2_FILLS = 0, 7
DN_FILL0, DN_FILLS = 7, 2
V_FILL0 = 9
PRE = V_FILL0 + NF
VT_FILL0 = PRE + NFILL
VT_BLOCKS = [(x, s, min(4, NJ - s)) for x in range(2) for s in range(0, NJ, 4)] + [(2, 0, 2)]
TILE1 = VT_FILL0 + len(VT_BLOCKS)
VT_ROWS = ROWS + (CROSS,)
BY_VECTOR = [n for n in range(TILE1) if (n < DN_FILL0 and n % 2) or (n >= VT_FILL0 and n % 2)]


def emptied_by_vector(n):
    return len([f for f in BY_VECTOR if f <= n])


def emptied_by_scalar(n):
    return n + 1 - emptied_by_vector(n)


def fills_before(t):
    return PRE if isinstance(t, int) and t == 0 else t * NFILL + (TILE1 - NFILL)


def emptied_s_at(t, m):
    if isinstance(t, int) and t == 0:
        return emptied_by_scalar(PRE + m)
    return t * NFILL + (TILE1 - NFILL + m + 1 - len(BY_VECTOR))


def dlrm_kernel(nc, dense, ids, tables, wt1, bt1, wt2, bt2, wt3, w1, b1, w2, b2, out):
    BATCH, DD = dense.shape
    NT = BATCH // P
    H1, H2 = wt1.shape[1], wt2.shape[1]
    C1, C2 = H1 // P, H2 // P
    assert NT % 2 == 0 and NT >= 4 and NFILL % RING == 0

    with ExitStack() as ctx:
        def sb(name, shape, dt=F32):
            return ctx.enter_context(nc.sbuf_tensor(name, shape, dt))

        def psum(name):
            return ctx.enter_context(nc.psum_tensor(name, [P, 512], F32))

        def sem(name):
            return ctx.enter_context(nc.semaphore(name))

        ids_sb = sb("ids_sb", [P, NT, NF], I32)
        ids_now = [sb(f"ids_now{i}", [P, NF], I32) for i in range(2)]
        emb = [sb(f"emb{i}", [P, NF * K]) for i in range(2)]
        xe = sb("xe", [P, XE * NS])
        pairs = sb("pairs", [P, NS, NP])
        bd = [sb(f"bd{i}", [P, NS, NJ, NG]) for i in range(2)]
        prod = sb("prod", [P, 2, NJ, P])
        cross_sb = sb("cross_sb", [CROSS, 2, P])
        v = sb("v", [P, NF * NV])
        w2_sb = v[:, NF * NV - P * NF:NF * NV].rearrange("h (i j) -> h i j", j=NF)
        w2t = sb("w2t", [P, NF, P])
        w1_sb = sb("w1_sb", [P, NF * NF])
        w1s = sb("w1s", [P, NV])
        vt = sb("vt", [P, NVT, P])
        ident = sb("ident", [P, P])
        wt1_sb = sb("wt1_sb", [P, 2, H1])
        wt1d_sb = sb("wt1d_sb", [DD, H1])
        wt2_sb = sb("wt2_sb", [P, C1, H2])
        wt3_sb = sb("wt3_sb", [P, C2])
        bt1_sb = sb("bt1_sb", [P, C1])
        bt2_sb = sb("bt2_sb", [P, C2])
        b2_sb = sb("b2_sb", [P, 1])
        b2k = sb("b2k", [P, 1])
        dense_sb = sb("dense_sb", [P, NT, DD])
        dense_t = sb("dense_t", [DD, BATCH])
        z_sb = sb("z_sb", [P, 2, P])
        h1_sb = sb("h1_sb", [P, C1, P])
        h2_sb = sb("h2_sb", [P, C2, P])
        y_sb = sb("y_sb", [1, BATCH])

        ring = [psum(f"ring{i}") for i in range(RING)]
        z_ps = psum("z_ps")
        h1_ps = psum("h1_ps")
        h2_ps = psum("h2_ps")

        ids_in = sem("ids_in")
        w1_in = sem("w1_in")
        w2_in = sem("w2_in")
        dense_in = sem("dense_in")
        mlp_in = sem("mlp_in")
        zeroed = sem("zeroed")
        ident_ready = sem("ident_ready")
        cleared_vec = sem("cleared_vec")
        ids_copied = sem("ids_copied")
        gathered = [[sem(f"gathered{i}{x}") for x in "aw"] for i in range(2)]
        emb_used = [sem(f"emb_used{i}") for i in range(2)]
        w1_folded = sem("w1_folded")
        v_folding = sem("v_folding")
        fills = sem("fills")
        emptied_s = sem("emptied_s")
        emptied_v = sem("emptied_v")
        xe_ready = [sem(f"xe_ready{x}") for x in "aw"]
        pairs_ready = [sem(f"pairs_ready{x}") for x in "aw"]
        bd_ready = sem("bd_ready")
        b2_scaled = sem("b2_scaled")
        z_done, z_ready = sem("z_done"), sem("z_ready")
        h1_done, h1_ready = sem("h1_done"), sem("h1_ready")
        h2_done, h2_ready = sem("h2_done"), sem("h2_ready")
        cross_in = sem("cross_in")
        y_done, y_ready = sem("y_done"), sem("y_ready")
        out_done = sem("out_done")

        def view(tensor, offset, dims, part=P):
            base = tensor[:]
            return bass.AP(tensor=base.tensor, offset=base.offset + offset,
                           ap=[[base.ap[0][0], part]] + [[s, c] for s, c in dims])

        def ring_of(n):
            return ring[n % RING]

        def tile_bank(t, m):
            return ring_of((PRE if isinstance(t, int) and t == 0 else TILE1) + m)

        block = ctx.enter_context(nc.Block())

        @block.sync
        def _(sp):
            sp.dma_start(ids_sb[:], ids.rearrange("(t p) f -> p t f", p=P)).then_inc(ids_in, 16)
            sp.dma_start(w2_sb, w2).then_inc(w2_in, 16)
            sp.dma_start(w1_sb[:], w1.rearrange("i p q -> i (p q)")).then_inc(w1_in, 16)
            with nc.allow_non_contiguous_dma(reason="one value per partition"):
                sp.dma_start(w1s[:, ONE:ONE + 1], b1.rearrange("(i o) -> i o", o=1)).then_inc(w1_in, 16)
            sp.dma_start(dense_sb[:], dense.rearrange("(t p) d -> p t d", p=P)).then_inc(dense_in, 16)
            sp.dma_start(wt1_sb[:], wt1[0:2 * P, :].rearrange("(c p) n -> p c n", p=P)).then_inc(mlp_in, 16)
            sp.dma_start(wt1d_sb[:], wt1[2 * P:2 * P + DD, :]).then_inc(mlp_in, 16)
            sp.dma_start(wt2_sb[:], wt2.rearrange("(c p) n -> p c n", p=P)).then_inc(mlp_in, 16)
            with nc.allow_non_contiguous_dma(reason="one value per partition"):
                sp.dma_start(wt3_sb[:], wt3.rearrange("(c p) o -> p (c o)", p=P)).then_inc(mlp_in, 16)
                sp.dma_start(bt1_sb[:], bt1.rearrange("(c p) -> p c", p=P)).then_inc(mlp_in, 16)
                sp.dma_start(bt2_sb[:], bt2.rearrange("(c p) -> p c", p=P)).then_inc(mlp_in, 16)
                sp.dma_start(b2_sb[:], b2.rearrange("(h o) -> h o", o=1)).then_inc(mlp_in, 16)

            def move_cross(t):
                sp.wait_ge(emptied_s, emptied_s_at(t, FILLS - 1))
                for w in range(NW):
                    r = w % CROSS_W * NA
                    sp.dma_start(cross_sb[r:r + NA, w // CROSS_W, :],
                                 prod[ONE_A:ONE_A + NA, 0, 1 + NA + w, :]).then_inc(cross_in, 16)

            move_cross(0)
            with sp.Fori(1, NT) as t:
                move_cross(t)
            sp.wait_ge(y_ready, NT)
            sp.dma_start(out.rearrange("b o -> o b"), y_sb[:]).then_inc(out_done, 16)
            sp.wait_ge(out_done, 16)

        @block.gpsimd
        def _(pool):
            nc.gpsimd.memset(ident[:], 0.0)
            nc.gpsimd.memset(bd[0][:], 0.0).then_inc(zeroed, 1)
            pool.wait_ge(zeroed, 1)
            nc.gpsimd.affine_select(out=ident[:], in_=ident[:], compare_op=ALU.not_equal, fill=1.0,
                                    base=0, pattern=[[-1, P]], channel_multiplier=1).then_inc(ident_ready, 1)
            pool.wait_ge(ids_in, 16)
            with pool.Fori(0, NT // 2) as i:
                for par in range(2):
                    pool.wait_ge(emb_used[par], i + 1)
                    nc.gpsimd.tensor_copy(ids_now[par][:], ids_sb[:, bass.ds(i * 2 + par, 1), :]
                                          ).then_inc(ids_copied, 1)
                    pool.wait_ge(ids_copied, i * 2 + par + 1)
                    pool.nop(nofuse=True)
                    for x in range(2):
                        for f in range(FIRST[x], FIRST[x] + SETS[x]):
                            pool.indirect_dma_start(
                                out=emb[par][:, K * f:K * f + K], out_offset=None, in_=tables[f][:, :],
                                in_offset=bass.IndirectOffsetOnAxis(
                                    ap=ids_now[par][:, f:f + 1].bitcast(U32), axis=0),
                            ).then_inc(gathered[par][x], 16)

        @block.vector
        def _(dve):
            nc.vector.memset(bd[1][:], 0.0).then_inc(cleared_vec, 1)
            nc.vector.memset(pairs[:, :, ONE:ONE + 1], 1.0)
            dve.wait_ge(cleared_vec, 1)
            dve.wait_ge(zeroed, 1)
            for par in range(2):
                for g in range(NG - 1):
                    nc.vector.memset(bd[par][K * g:K * g + K, :, 0, g], 1.0)
                nc.vector.memset(bd[par][K * (NG - 1):P, :, 0, NG - 1], 1.0).then_inc(emb_used[par], 1)

            nc.vector.memset(w1s[:, ONE_A:AA], 0.0)
            dve.wait_ge(w1_in, 32)
            for x, c0 in ((0, AA), (1, WW)):
                for d, p, q, m in shifts(SETS[x]):
                    dst = view(w1s, c0 + d * SETS[x] + p, [(1, m)])
                    pq = view(w1_sb, (FIRST[x] + p) * NF + FIRST[x] + q, [(NF + 1, m)])
                    qp = view(w1_sb, (FIRST[x] + q) * NF + FIRST[x] + p, [(NF + 1, m)])
                    if d == 0:
                        nc.vector.tensor_copy(dst, pq)
                    else:
                        nc.vector.tensor_tensor(dst, pq, qp, ALU.add)
            nc.vector.tensor_tensor(view(w1s, AW, [(NA, NW), (1, NA)]),
                                    view(w1_sb, NA, [(1, NW), (NF, NA)]),
                                    view(w1_sb, NA * NF, [(NF, NW), (1, NA)]), ALU.add
                                    ).then_inc(w1_folded, 1)

            for n in range(1, W2_FILLS, 2):
                dve.wait_ge(fills, n + 1)
                m = min(4, NF - 4 * n)
                nc.vector.tensor_copy(w2t[:, 4 * n:4 * n + m, :].rearrange("i j h -> i (j h)"),
                                      ring_of(n)[:, 0:m * P]).then_inc(emptied_v, 1)

            def transpose_set(x, t, par):
                dve.wait_ge(gathered[par][x], (t + (2 - par)) * (8 * SETS[x]))
                if x == 0:
                    dve.wait_ge(bd_ready, t)
                    dve.wait_ge(pairs_ready[1], t)
                src = emb[par][:, K * FIRST[x]:K * (FIRST[x] + SETS[x])]
                nc.vector.transpose(xe[:, XE0[x] * NS:(XE0[x] + SETS[x]) * NS], src)
                w0 = XE0[x] + SETS[x]
                last = nc.vector.transpose(xe[:, w0 * NS:(w0 + WRAP[x]) * NS], src[:, 0:K * WRAP[x]])
                last.then_inc(xe_ready[x], 1)
                dve.wait_ge(xe_ready[x], t + 1)

            def within(col, n, f, d0, nd, m):
                return nc.vector.tensor_tensor(
                    view(pairs, col + d0 * n, [(NP, NS), (n, nd), (1, m)]),
                    view(xe, f * NS, [(1, NS), (0, nd), (NS, m)]),
                    view(xe, (f + d0) * NS, [(1, NS), (NS, nd), (NS, m)]), ALU.mult)

            def form_pairs(x, t, par):
                transpose_set(x, t, par)
                if not (isinstance(t, int) and t == 0):
                    dve.wait_ge(fills, fills_before(t) - NFILL + (x + 1) * FILLS)
                if x == 0:
                    nc.vector.tensor_copy(view(pairs, ONE_A, [(NP, NS), (1, NA)]),
                                          view(xe, XE0[0] * NS, [(1, NS), (NS, NA)]))
                n, col = SETS[x], (AA, WW)[x]
                mm = within(col, n, XE0[x], n // 2, 1, n // 2)
                if x == 1:
                    mm.then_inc(emb_used[par], 1)
                within(col, n, XE0[x], 0, n // 2, n).then_inc(pairs_ready[x], 1)

            def fold(dst_j, dst_col, dst_dims, src_j, src_col, src_dims):
                dst = view(v, dst_j * NV + dst_col, dst_dims)
                return nc.vector.tensor_tensor(dst, dst, view(v, src_j * NV + src_col, src_dims), ALU.add)

            def fold_v():
                dve.wait_ge(emptied_s, emptied_by_scalar(V_FILL0 + NF - 1))
                for half in range(2):
                    if half:
                        dve.wait_ge(v_folding, 1)
                    for d, p, q, m in shifts(NA):
                        if half and d == 0:
                            continue
                        j, a = ((p, q), (q, p))[half]
                        fold(NA, AA + d * NA + p, [(NV, NW), (1, m)], j, AW + a, [(NA, NW), (NV + 1, m)])
                    for d, p, q, m in shifts(NW):
                        if half and d == 0:
                            continue
                        j, w = ((p, q), (q, p))[half]
                        last = fold(0, WW + d * NW + p, [(NV, NA), (1, m)],
                                    NA + j, AW + w * NA, [(1, NA), (NV + NA, m)])
                    last.then_inc(v_folding, 1)

            form_pairs(0, 0, 0)
            form_pairs(1, 0, 0)
            fold_v()
            for n in [f for f in BY_VECTOR if f >= VT_FILL0]:
                x, b, m = VT_BLOCKS[n - VT_FILL0]
                b += (0, NJ, VT_CROSS)[x]
                dve.wait_ge(fills, n + 1)
                nc.vector.tensor_copy(vt[0:VT_ROWS[x], b:b + m, :].rearrange("r j h -> r (j h)"),
                                      ring_of(n)[0:VT_ROWS[x], 0:m * P]).then_inc(emptied_v, 1)
            with dve.Fori(1, NT - 1, 2) as t:
                for u in range(2):
                    form_pairs(0, t + u, 1 - u)
                    form_pairs(1, t + u, 1 - u)
            form_pairs(0, NT - 1, 1)
            form_pairs(1, NT - 1, 1)

        @block.scalar
        def _(act):
            def copy(dst, src):
                return nc.scalar.activation(dst, src, ACT.Copy)

            def fill_block_diagonal(x, t, par):
                act.wait_ge(xe_ready[x], t + 1)
                for g in range(NG):
                    rows = slice(K * g, K * g + K)
                    last = copy(bd[par][rows, :, 1 + FIRST[x]:1 + FIRST[x] + SETS[x], g],
                                xe[rows, XE0[x] * NS:(XE0[x] + SETS[x]) * NS].rearrange(
                                    "p (f s) -> p s f", s=NS))
                if x == 1:
                    last.then_inc(bd_ready, 1)

            def empty_products(t, m0, m1):
                for m in range(m0, m1):
                    x = m // FILLS
                    act.wait_ge(fills, fills_before(t) + (m + 1))
                    src = tile_bank(t, m)[0:ROWS[x], 0:PER * NJ * NG]
                    dst = view(prod, x * NJ * P + m % FILLS * PER, [(1, PER), (P, NJ), (NS, NG)], ROWS[x])
                    copy(dst, src.rearrange("r (u j g) -> r u j g", g=NG, j=NJ)).then_inc(emptied_s, 1)

            def empty_h1(t):
                act.wait_ge(h1_done, t + 1)
                for c in range(C1):
                    last = nc.scalar.activation(h1_sb[:, c, :], h1_ps[:, P * c:P * c + P], ACT.Relu,
                                                bias=bt1_sb[:, c:c + 1])
                last.then_inc(h1_ready, 1)

            def empty_h2(t):
                act.wait_ge(h2_done, t + 1)
                for c in range(C2):
                    last = nc.scalar.activation(h2_sb[:, c, :], h2_ps[:, P * c:P * c + P], ACT.Relu,
                                                bias=bt2_sb[:, c:c + 1])
                last.then_inc(h2_ready, 1)

            def empty_y(t):
                act.wait_ge(y_done, t + 1)
                copy(y_sb[:, bass.ds(t * P, P)], h2_ps[0:1, C2 * P:C2 * P + P]).then_inc(y_ready, 1)

            def empty_z(t):
                act.wait_ge(z_done, t + 1)
                copy(z_sb[:, 0, :], z_ps[:, P:2 * P])
                nc.scalar.activation(z_sb[:, 1, :], z_ps[:, 0:P], ACT.Identity,
                                     bias=b2k[:, 0:1]).then_inc(z_ready, 1)

            def empty_vt():
                for n in range(VT_FILL0, TILE1):
                    if n in BY_VECTOR:
                        continue
                    x, b, m = VT_BLOCKS[n - VT_FILL0]
                    b += (0, NJ, VT_CROSS)[x]
                    act.wait_ge(fills, n + 1)
                    copy(vt[0:VT_ROWS[x], b:b + m, :].rearrange("r j h -> r (j h)"),
                         ring_of(n)[0:VT_ROWS[x], 0:m * P]).then_inc(emptied_s, 1)

            def tile(t, par, first=False, last=False):
                empty_products(t, 0, FILLS)
                if not first:
                    empty_h1(t - 1)
                empty_products(t, FILLS, LATE)
                if not first:
                    empty_h2(t - 1)
                empty_products(t, LATE, NFILL)
                if first:
                    empty_vt()
                else:
                    empty_y(t - 1)
                if not last:
                    fill_block_diagonal(0, t + 1, 1 - par)
                empty_z(t)
                if not last:
                    fill_block_diagonal(1, t + 1, 1 - par)

            for n in range(0, W2_FILLS, 2):
                act.wait_ge(fills, n + 1)
                m = min(4, NF - 4 * n)
                copy(w2t[:, 4 * n:4 * n + m, :].rearrange("i j h -> i (j h)"),
                     ring_of(n)[:, 0:m * P]).then_inc(emptied_s, 1)
            for n in range(DN_FILLS):
                act.wait_ge(fills, DN_FILL0 + n + 1)
                copy(dense_t[:, 4 * P * n:4 * P * n + 4 * P], ring_of(DN_FILL0 + n)[0:DD, :]
                     ).then_inc(emptied_s, 1)
            for j in range(NF):
                act.wait_ge(fills, V_FILL0 + j + 1)
                copy(v[:, j * NV:j * NV + NV], ring_of(V_FILL0 + j)[:, 0:NV]).then_inc(emptied_s, 1)
            act.wait_ge(mlp_in, 7 * 16)
            nc.scalar.mul(b2k[:], b2_sb[:], float(K)).then_inc(b2_scaled, 1)
            act.wait_ge(emb_used[0], 1)
            act.wait_ge(emb_used[1], 1)
            fill_block_diagonal(0, 0, 0)
            fill_block_diagonal(1, 0, 0)
            act.wait_ge(b2_scaled, 1)
            tile(0, 0, first=True)
            with act.Fori(1, NT - 1, 2) as t:
                for u in range(2):
                    tile(t + u, 1 - u)
            tile(NT - 1, 1, last=True)
            empty_h1(NT - 1)
            empty_h2(NT - 1)
            empty_y(NT - 1)

        @block.tensor
        def _(pe):
            def early_slot(n):
                if n >= RING:
                    if n - RING in BY_VECTOR:
                        pe.wait_ge(emptied_v, emptied_by_vector(n - RING))
                    else:
                        pe.wait_ge(emptied_s, emptied_by_scalar(n - RING))

            def products(t, par, m0, m1):
                for m in range(m0, m1):
                    x = m // FILLS
                    if m % FILLS == 0:
                        pe.wait_ge(pairs_ready[x], t + 1)
                        pe.wait_ge(bd_ready, t + 1)
                    pe.wait_ge(emptied_s, emptied_s_at(t, m - RING))
                    for u in range(PER):
                        s = m % FILLS * PER + u
                        mm = pe.matmul(tile_bank(t, m)[0:ROWS[x], u * NJ * NG:(u + 1) * NJ * NG],
                                       pairs[:, s, ROW0[x]:ROW0[x] + ROWS[x]],
                                       bd[par][:, s].rearrange("p j g -> p (j g)"), start=True, stop=True)
                    mm.then_inc(fills, 1)

            def interactions(t):
                pe.wait_ge(emptied_s, emptied_s_at(t, NFILL - 1))
                for x in range(2):
                    for s in range(1, NJ):
                        pe.matmul(z_ps[:, 0:P], vt[0:ROWS[x], VT0[x] + s, :], prod[0:ROWS[x], x, s, :],
                                  start=(x, s) == (0, 1), stop=(x, s) == (1, NJ - 1))
                for x in range(2):
                    pe.matmul(z_ps[:, P:2 * P], vt[0:ROWS[x], VT0[x], :], prod[0:ROWS[x], x, 0, :],
                              start=x == 0, stop=False)
                pe.wait_ge(cross_in, (t + 1) * (16 * NW))
                for c in range(2):
                    mm = pe.matmul(z_ps[:, P:2 * P], vt[0:CROSS, VT_CROSS + c, :], cross_sb[:, c, :],
                                   start=False, stop=c == 1)
                mm.then_inc(z_done, 1)

            def layer1(t):
                pe.wait_ge(z_ready, t + 1)
                for c in range(C1):
                    cols = slice(P * c, P * c + P)
                    pe.matmul(h1_ps[:, cols], wt1_sb[:, 0, cols], z_sb[:, 0, :], start=True, stop=False)
                    pe.matmul(h1_ps[:, cols], wt1_sb[:, 1, cols], z_sb[:, 1, :], start=False, stop=False)
                    mm = pe.matmul(h1_ps[:, cols], wt1d_sb[:, cols], dense_t[:, bass.ds(t * P, P)],
                                   start=False, stop=True)
                mm.then_inc(h1_done, 1)

            def layer2(t):
                pe.wait_ge(h1_ready, t + 1)
                for c in range(C2):
                    for k in range(C1):
                        mm = pe.matmul(h2_ps[:, P * c:P * c + P], wt2_sb[:, k, P * c:P * c + P],
                                       h1_sb[:, k, :], start=(k == 0), stop=(k == C1 - 1))
                mm.then_inc(h2_done, 1)

            def layer3(t):
                pe.wait_ge(h2_ready, t + 1)
                for k in range(C2):
                    mm = pe.matmul(h2_ps[0:1, C2 * P:C2 * P + P], wt3_sb[:, k:k + 1], h2_sb[:, k, :],
                                   start=(k == 0), stop=(k == C2 - 1))
                mm.then_inc(y_done, 1)

            def turn_v():
                pe.wait_ge(v_folding, 2)
                for k, (x, b, m) in enumerate(VT_BLOCKS):
                    early_slot(VT_FILL0 + k)
                    for u in range(m):
                        if x == 2:
                            src = w1s[:, AW + u * CROSS:AW + (u + 1) * CROSS]
                        elif b + u == 0:
                            src = w1s[:, ROW0[x]:ROW0[x] + ROWS[x]]
                        else:
                            c = (b + u - 1) * NV + ROW0[x]
                            src = v[:, c:c + ROWS[x]]
                        mm = pe.transpose(ring_of(VT_FILL0 + k)[0:VT_ROWS[x], P * u:P * u + P], src, ident[:])
                    mm.then_inc(fills, 1)
                pe.wait_ge(emptied_v, emptied_by_vector(TILE1 - 1))
                pe.wait_ge(emptied_s, emptied_by_scalar(TILE1 - 1))
                pe.wait_ge(mlp_in, 7 * 16)

            def tile(t, par, first=False):
                products(t, par, 0, FILLS)
                if not first:
                    layer1(t - 1)
                products(t, par, FILLS, LATE)
                if not first:
                    layer2(t - 1)
                products(t, par, LATE, NFILL)
                if first:
                    turn_v()
                else:
                    layer3(t - 1)
                interactions(t)

            pe.wait_ge(ident_ready, 1)
            pe.wait_ge(w2_in, 16)
            for n in range(W2_FILLS):
                early_slot(n)
                for u in range(min(4, NF - 4 * n)):
                    mm = pe.transpose(ring_of(n)[:, P * u:P * u + P], w2_sb[:, :, 4 * n + u], ident[:])
                mm.then_inc(fills, 1)
            pe.wait_ge(dense_in, 16)
            for n in range(DN_FILLS):
                early_slot(DN_FILL0 + n)
                for u in range(4):
                    mm = pe.transpose(ring_of(DN_FILL0 + n)[0:DD, P * u:P * u + P],
                                      dense_sb[:, 4 * n + u, :], ident[:])
                mm.then_inc(fills, 1)
            pe.wait_ge(w1_folded, 1)
            pe.wait_ge(emptied_v, emptied_by_vector(W2_FILLS - 1))
            pe.wait_ge(emptied_s, emptied_by_scalar(W2_FILLS - 1))
            for j in range(NF):
                early_slot(V_FILL0 + j)
                pe.matmul(ring_of(V_FILL0 + j)[:, 0:NV], w2t[:, j, :], w1s[:],
                          start=True, stop=True).then_inc(fills, 1)
            tile(0, 0, first=True)
            with pe.Fori(1, NT - 1, 2) as t:
                for u in range(2):
                    tile(t + u, 1 - u)
            tile(NT - 1, 1)
            layer1(NT - 1)
            layer2(NT - 1)
            layer3(NT - 1)


def kernel(**inputs):
    import numpy as np
    import concourse.bacc as bacc
    from concourse.bass_utils import run_bass_kernel_spmd

    nc = bacc.Bacc("TRN2", target_bir_lowering=False, num_devices=1)
    arrays = {}

    def dram(name):
        a = np.ascontiguousarray(inputs[name])
        arrays[f"in_{name}"] = a
        return nc.dram_tensor(f"in_{name}", a.shape, mybir.dt.from_np(a.dtype), kind="ExternalInput").ap()

    tables = [dram(f"tbl_{f}") for f in range(26)]
    dense, ids = dram("dense_ctx"), dram("ids")
    mlp = [dram(n) for n in ("W_top1", "b_top1", "W_top2", "b_top2", "W_top3")]
    cin = [dram(n) for n in ("L0_rec_W1", "L0_rec_b1", "L0_rec_W2", "L0_rec_b2")]
    out = nc.dram_tensor("out_y", (dense.shape[0], 1), F32, kind="ExternalOutput").ap()
    dlrm_kernel(nc, dense, ids, tables, *mlp, *cin, out)
    r = run_bass_kernel_spmd(nc, [arrays], core_ids=[0])
    return r.results[0]["out_y"]
```

```python
from contextlib import ExitStack

import concourse.bass as bass
from concourse import mybir

F32 = mybir.dt.float32
F32R = mybir.dt.float32r
I32 = mybir.dt.int32
U32 = mybir.dt.uint32
ALU = mybir.AluOpType
ACT = mybir.ActivationFunctionType

P = 128
NF = 26
K = 32
NJ = NF + 1
NG = P // K
NS = P // NG
SETS = (13, 13)
FIRST = (0, 13)
NA, NW = SETS
ONE_SLOT = NA
FIRST_SLOT = (0, NA + 1)


def shifts(n):
    runs = [(0, 0, 0, n)]
    for d in range(1, (n + 1) // 2):
        runs += [(d, 0, d, n - d), (d, n - d, 0, d)]
    if n % 2 == 0:
        runs.append((n // 2, 0, n // 2, n // 2))
    return runs


AA = 0
ONE = NA * (NA + 1) // 2
ONE_A = ONE + 1
WW = ONE_A + NA
ROWS = (WW, NW * (NW + 1) // 2)
ROW0 = (0, WW)
NP = sum(ROWS)
AW = NP
NV = NP + NW * NA
assert max(ROWS) <= P and NV <= 512

WRAP = (NA // 2, NW // 2)
XE0 = (0, NA + WRAP[0])
XE = XE0[1] + NW + WRAP[1]

HALF = P // 2
SHARED = ((NA + 1) // 2, (NW + 1) // 2)


def kept_products(n, slot0, col0):
    def row(p, q):
        d = (q - p) % n
        return d * n + p if d <= n // 2 else (n - d) * n + q
    taken, moves = {}, []
    for r in range(HALF, n * (n + 1) // 2):
        d, p = divmod(r, n)
        q = (p + d) % n
        for e in range(n):
            j = (p + e) % n
            r2, k = min((row(p, j), q), (row(q, j), p))
            assert r2 < HALF
            to = k * NV + r2
            taken[to] = taken.get(to, 0) + 1
            moves.append((taken[to], e, r, j * NV + r, to))
    base = slot0 * NV + col0
    runs = []
    for rnd, e, r, a, b in sorted(moves):
        a, b = a + base, b + base
        if runs and runs[-1][0] == rnd:
            _, a0, da, b0, db, m = runs[-1]
            if m == 1 and a > a0 and b > b0:
                runs[-1] = (rnd, a0, a - a0, b0, b - b0, 2)
                continue
            if m > 1 and (a, b) == (a0 + m * da, b0 + m * db):
                runs[-1] = (rnd, a0, da, b0, db, m + 1)
                continue
        runs.append((rnd, a, 1, b, 1, 1))
    assert max(run[0] for run in runs) == ROUNDS
    return runs


VT0 = (0, NA + 1)
VT_ONE = (0, 2 * NA + 1)
VT_SHARED = (2 * NA + 2, 2 * NA + 2 + SHARED[0])
VT_CROSS = VT_SHARED[1] + SHARED[1]
VT_LINEAR = VT_CROSS + 2
NVT = VT_LINEAR + 1
ROUNDS = 2
CROSS_W = (NW + 1) // 2
CROSS = (CROSS_W * NA, (NW - CROSS_W) * NA)
assert NA == NW and NA % 2


def block_rows(b):
    if b < VT_SHARED[0]:
        return ROWS[b > NW]
    if b < VT_CROSS:
        return HALF if b in (VT_SHARED[1] - 1, VT_CROSS - 1) else P
    return CROSS[b - VT_CROSS] if b < VT_LINEAR else ROWS[0]


def block_limit(b):
    return 2 if VT_SHARED[0] <= b < VT_CROSS else 4


def block_runs(*ranges):
    runs = []
    for lo, hi in ranges:
        while lo < hi:
            m = 1
            while m < block_limit(lo) and lo + m < hi and block_rows(lo + m) == block_rows(lo):
                m += 1
            runs.append((lo, m))
            lo += m
    return runs


PER = 4
FILLS = NS // PER
NFILL = 2 * FILLS
RING = 4

VT_OF_W1 = block_runs((VT_ONE[0], VT_ONE[0] + 1), (VT_ONE[1], VT_ONE[1] + 1), (VT_CROSS, VT_LINEAR))
VT_OF_A = block_runs((VT_SHARED[0], VT_SHARED[1]))
VT_OF_W = block_runs((VT_SHARED[1], VT_CROSS), (VT_LINEAR, NVT))
VT_AA_W = block_runs((VT0[0] + 1, VT0[1]))
VT_WW_A = block_runs((VT0[1], VT_ONE[1]))
VT_LATER = VT_OF_W + VT_AA_W + VT_WW_A
FOLDED = {"A": 2, "W": 4, "AA with w": 6, "WW with a": 8}


def v_and_runs():
    order, runs = [], list(VT_OF_W1)
    for j in range(NF):
        order.append(j)
        if j >= NF // 2 and runs:
            order.append(runs.pop(0))
    return order + runs + VT_OF_A


DN_FILL0, DN_FILLS = 0, 2
W2_FILL0, W2_FILLS = 2, 7
V_FILL0 = W2_FILL0 + W2_FILLS
EARLY = v_and_runs()
V_FILL = [V_FILL0 + EARLY.index(j) for j in range(NF)]
PRE = V_FILL0 + len(EARLY)
ADDED_FILL0 = PRE + NFILL
TILE1 = ADDED_FILL0 + len(VT_LATER)


def vt_run(n):
    if V_FILL0 <= n < PRE:
        return EARLY[n - V_FILL0] if isinstance(EARLY[n - V_FILL0], tuple) else None
    return VT_LATER[n - ADDED_FILL0] if ADDED_FILL0 <= n < TILE1 else None


BY_VECTOR = [n for n in range(TILE1) if n < DN_FILLS or (n % 2 and n < V_FILL0) or
             (PRE - len(VT_OF_A) <= n < PRE and n % 2)]
BD_BY_SCALAR = 2


def emptied_by_vector(n):
    return len([f for f in BY_VECTOR if f <= n])


def emptied_by_scalar(n):
    return n + 1 - emptied_by_vector(n)


def fills_before(t):
    return PRE if isinstance(t, int) and t == 0 else t * NFILL + (TILE1 - NFILL)


def emptied_s_at(t, m):
    if isinstance(t, int) and t == 0:
        return emptied_by_scalar(PRE + m)
    return t * NFILL + (TILE1 - NFILL + m + 1 - len(BY_VECTOR))


def dlrm_kernel(nc, dense, ids, tables, wt1, bt1, wt2, bt2, wt3, w1, b1, w2, b2, out):
    BATCH, DD = dense.shape
    NT = BATCH // P
    H1, H2 = wt1.shape[1], wt2.shape[1]
    C1, C2 = H1 // P, H2 // P
    MLP_LOADS = 6 + NG
    assert NT % 2 == 0 and NT >= 4 and NFILL % RING == 0 and NT == 4 * DN_FILLS and DD <= K

    with ExitStack() as ctx:
        def sb(name, shape, dt=F32):
            return ctx.enter_context(nc.sbuf_tensor(name, shape, dt))

        def psum(name):
            return ctx.enter_context(nc.psum_tensor(name, [P, 512], F32))

        def sem(name):
            return ctx.enter_context(nc.semaphore(name))

        ids_sb = sb("ids_sb", [P, NT, NF], I32)
        ids_now = [sb(f"ids_now{i}", [P, NF], I32) for i in range(2)]
        emb = [sb(f"emb{i}", [P, NF * K]) for i in range(2)]
        xe = sb("xe", [P, XE * NS])
        pairs = sb("pairs", [P, NS, NP])
        bd = [sb(f"bd{i}", [P, NS, NJ, NG]) for i in range(2)]
        prod = sb("prod", [P, 2, NA + 1, P])
        prod_shared = sb("prod_shared", [P, 2, SHARED[0], P])
        linear = sb("linear", [P, ROWS[0]])
        cross_sb = sb("cross_sb", [max(CROSS), 2, P])
        w2t = sb("w2t", [P, NF, P])
        w1_sb = sb("w1_sb", [P, NF * NF])
        w1s = sb("w1s", [P, NV])
        vt = sb("vt", [P, NVT, P])
        ident = sb("ident", [P, P])
        wt1_sb = sb("wt1_sb", [P, 2, H1])
        wt1d_sb = sb("wt1d_sb", [P, H1])
        wt2_sb = sb("wt2_sb", [P, C1, H2])
        wt3_sb = sb("wt3_sb", [P, C2])
        bt1_sb = sb("bt1_sb", [P, C1])
        bt2_sb = sb("bt2_sb", [P, C2])
        b2_sb = sb("b2_sb", [P, 1])
        b2k = sb("b2k", [P, 1])
        dense_sb = sb("dense_sb", [P, NT, DD])
        dense4 = prod[:, 0, 0:NT, :]
        dense_t = sb("dense_t", [P, BATCH], F32R)
        z_sb = sb("z_sb", [P, 2, P])
        h1_sb = sb("h1_sb", [P, C1, P])
        h2_sb = sb("h2_sb", [P, C2, P])
        y_sb = sb("y_sb", [1, BATCH])

        v = sb("v", [P, NF * NV])
        w2_sb = v[:, NF * NV - P * NF:NF * NV].rearrange("h (i j) -> h i j", j=NF)
        wt1d = sb("wt1d", [P, H1], F32R)

        ring = [psum(f"ring{i}") for i in range(RING)]
        z_ps = psum("z_ps")
        h1_ps = psum("h1_ps")
        h2_ps = psum("h2_ps")
        assert H1 == 4 * P and H2 == 2 * P

        ids_in = sem("ids_in")
        w1_in = sem("w1_in")
        w2_in = sem("w2_in")
        dense_in = sem("dense_in")
        mlp_in = sem("mlp_in")
        ident_cleared = sem("ident_cleared")
        ident_ready = sem("ident_ready")
        cleared_vec = sem("cleared_vec")
        ones_set = sem("ones_set")
        ids_ready = [sem(f"ids_ready{i}") for i in range(2)]
        gathered = [[sem(f"gathered{i}{x}") for x in "aw"] for i in range(2)]
        w1_folded = sem("w1_folded")
        v_folding = sem("v_folding")
        fills = sem("fills")
        emptied_s = sem("emptied_s")
        emptied_v = sem("emptied_v")
        xe_ready = [sem(f"xe_ready{x}") for x in "aw"]
        wrapped = [sem(f"wrapped{x}") for x in "aw"]
        pairs_ready = [sem(f"pairs_ready{x}") for x in "aw"]
        bd_ready = sem("bd_ready")
        bd_by_vector = sem("bd_by_vector")
        b2_scaled = sem("b2_scaled")
        dense_spread = sem("dense_spread")
        dense_hi = sem("dense_hi")
        dense_split = sem("dense_split")
        weights_hi = sem("weights_hi")
        z_done, z_ready = sem("z_done"), sem("z_ready")
        h1_done, h1_ready = sem("h1_done"), sem("h1_ready")
        h2_done, h2_ready = sem("h2_done"), sem("h2_ready")
        cross_in = sem("cross_in")
        last_h1_done, last_h1_out = sem("last_h1_done"), sem("last_h1_out")
        last_h2_out = sem("last_h2_out")
        y_done, y_ready = sem("y_done"), sem("y_ready")
        out_done = sem("out_done")

        def view(tensor, offset, dims, part=P):
            base = tensor[:]
            return bass.AP(tensor=base.tensor, offset=base.offset + offset,
                           ap=[[base.ap[0][0], part]] + [[s, c] for s, c in dims])

        def ring_of(n):
            return ring[n % RING]

        def tile_bank(t, m):
            return ring_of((PRE if isinstance(t, int) and t == 0 else TILE1) + m)

        def w2_fields(n):
            return min(4, NF - 4 * (n - W2_FILL0))

        def w2t_of(n):
            j = 4 * (n - W2_FILL0)
            return w2t[:, j:j + w2_fields(n), :].rearrange("i j h -> i (j h)")

        def weight_parts(n):
            b, m = vt_run(n)
            rows = block_rows(b)
            if block_limit(b) == 4:
                return [(vt[0:rows, b:b + m, :], ring_of(n)[0:rows, 0:m * P].rearrange("r (j h) -> r j h", h=P))]
            slots = rows // HALF * m
            bank = ring_of(n)[0:HALF, 0:slots * P].rearrange("r (j h) -> r j h", h=P)
            return [(vt[HALF * odd:HALF * odd + HALF, b:b + m, :], bank[:, odd:slots:rows // HALF, :])
                    for odd in range(rows // HALF)]

        y_part = h2_ps[0:1, C2 * P:C2 * P + P]

        last_h2_ps = (h2_ps, h1_ps)

        def bd_part(par, x, g):
            return bd[par][K * g:K * g + K, :, FIRST_SLOT[x]:FIRST_SLOT[x] + SETS[x], g]

        def xe_part(x, g):
            return xe[K * g:K * g + K, XE0[x] * NS:(XE0[x] + SETS[x]) * NS].rearrange(
                "p (f s) -> p s f", s=NS)

        block = ctx.enter_context(nc.Block())

        @block.sync
        def _(sp):
            sp.dma_start(ids_sb[:], ids.rearrange("(t p) f -> p t f", p=P)).then_inc(ids_in, 16)
            sp.dma_start(dense_sb[:], dense.rearrange("(t p) d -> p t d", p=P)).then_inc(dense_in, 16)
            sp.dma_start(w2_sb, w2).then_inc(w2_in, 16)
            sp.dma_start(w1_sb[:], w1.rearrange("i p q -> i (p q)")).then_inc(w1_in, 16)
            with nc.allow_non_contiguous_dma(reason="one value per partition"):
                sp.dma_start(w1s[:, ONE:ONE + 1], b1.rearrange("(i o) -> i o", o=1)).then_inc(w1_in, 16)
            sp.dma_start(wt1_sb[:], wt1[0:2 * P, :].rearrange("(c p) n -> p c n", p=P)).then_inc(mlp_in, 16)
            sp.dma_start(wt2_sb[:], wt2.rearrange("(c p) n -> p c n", p=P)).then_inc(mlp_in, 16)
            with nc.allow_non_contiguous_dma(reason="one value per partition"):
                sp.dma_start(wt3_sb[:], wt3.rearrange("(c p) o -> p (c o)", p=P)).then_inc(mlp_in, 16)
                sp.dma_start(bt1_sb[:], bt1.rearrange("(c p) -> p c", p=P)).then_inc(mlp_in, 16)
                sp.dma_start(bt2_sb[:], bt2.rearrange("(c p) -> p c", p=P)).then_inc(mlp_in, 16)
                sp.dma_start(b2_sb[:], b2.rearrange("(h o) -> h o", o=1)).then_inc(mlp_in, 16)
            sp.wait_ge(cleared_vec, 2)
            for g in range(NG):
                sp.dma_start(wt1d_sb[K * g:K * g + DD, :], wt1[2 * P:2 * P + DD, :]).then_inc(mlp_in, 16)

            def move_cross(t):
                sp.wait_ge(emptied_s, emptied_s_at(t, FILLS - 1))
                for w in range(NW):
                    r = w % CROSS_W * NA
                    sp.dma_start(cross_sb[r:r + NA, w // CROSS_W, :],
                                 prod[ONE_A:ONE_A + NA, 0, 1 + w, :]).then_inc(cross_in, 16)

            move_cross(0)
            with sp.Fori(1, NT) as t:
                move_cross(t)
            sp.wait_ge(y_ready, NT)
            sp.dma_start(out.rearrange("b o -> o b"), y_sb[:]).then_inc(out_done, 16)
            sp.wait_ge(out_done, 16)

        @block.gpsimd
        def _(pool):
            nc.gpsimd.memset(ident[:], 0.0).then_inc(ident_cleared, 1)
            pool.wait_ge(ident_cleared, 1)
            nc.gpsimd.affine_select(out=ident[:], in_=ident[:], compare_op=ALU.not_equal, fill=1.0,
                                    base=0, pattern=[[-1, P]], channel_multiplier=1).then_inc(ident_ready, 1)
            pool.wait_ge(ids_in, 16)
            with pool.Fori(0, NT // 2) as i:
                for par in range(2):
                    pool.wait_ge(ids_ready[par], i + 1)
                    pool.nop(nofuse=True)
                    for x in range(2):
                        for f in range(FIRST[x], FIRST[x] + SETS[x]):
                            pool.indirect_dma_start(
                                out=emb[par][:, K * f:K * f + K], out_offset=None, in_=tables[f][:, :],
                                in_offset=bass.IndirectOffsetOnAxis(
                                    ap=ids_now[par][:, f:f + 1].bitcast(U32), axis=0),
                            ).then_inc(gathered[par][x], 16)

        @block.vector
        def _(dve):
            def split_dense():
                low = slice(2 * K, P)
                for n in range(DN_FILLS):
                    dve.wait_ge(dense_hi, n + 1)
                    part = dense_t[low, 4 * P * n:4 * P * n + 4 * P]
                    nc.vector.tensor_tensor(part, ring_of(DN_FILL0 + n)[low, :], part.bitcast(F32),
                                            ALU.subtract).then_inc(emptied_v, 1)

            def copy_ids(t, par):
                nc.vector.tensor_copy(ids_now[par][:], ids_sb[:, bass.ds(t, 1), :]).then_inc(ids_ready[par], 1)

            nc.vector.memset(dense4, 0.0).then_inc(cleared_vec, 1)
            nc.vector.memset(pairs[:, :, ONE:ONE + 1], 1.0)
            dve.wait_ge(ids_in, 16)
            for t in range(2):
                copy_ids(t, t)
            dve.wait_ge(cleared_vec, 1)
            dve.wait_ge(dense_in, 16)
            for g in range(NG):
                last = nc.vector.tensor_copy(dense4[:, :, K * g:K * g + DD], dense_sb[:])
            last.then_inc(dense_spread, 1)
            nc.vector.memset(wt1d_sb[:], 0.0).then_inc(cleared_vec, 1)

            def prepare_bd(par):
                nc.vector.memset(bd[par][:], 0.0).then_inc(cleared_vec, 1)
                dve.wait_ge(cleared_vec, 3 + par)
                for g in range(NG):
                    nc.vector.memset(bd[par][K * g:K * g + K, :, ONE_SLOT, g], 1.0).then_inc(ones_set, 1)

            prepare_bd(0)
            split_dense()
            nc.vector.memset(w1s[:, ONE_A:WW], 0.0)
            dve.wait_ge(w1_in, 32)
            for x, c0 in ((0, AA), (1, WW)):
                for d, p, q, m in shifts(SETS[x]):
                    dst = view(w1s, c0 + d * SETS[x] + p, [(1, m)])
                    pq = view(w1_sb, (FIRST[x] + p) * NF + FIRST[x] + q, [(NF + 1, m)])
                    qp = view(w1_sb, (FIRST[x] + q) * NF + FIRST[x] + p, [(NF + 1, m)])
                    if d == 0:
                        nc.vector.tensor_copy(dst, pq)
                    else:
                        nc.vector.tensor_tensor(dst, pq, qp, ALU.add)
            nc.vector.tensor_tensor(view(w1s, AW, [(NA, NW), (1, NA)]),
                                    view(w1_sb, NA, [(1, NW), (NF, NA)]),
                                    view(w1_sb, NA * NF, [(NF, NW), (1, NA)]), ALU.add
                                    ).then_inc(w1_folded, 1)

            for n in [f for f in BY_VECTOR if W2_FILL0 <= f < V_FILL0]:
                dve.wait_ge(fills, n + 1)
                nc.vector.tensor_copy(w2t_of(n), ring_of(n)[:, 0:w2_fields(n) * P]).then_inc(emptied_v, 1)
            prepare_bd(1)

            def transpose_set(x, t, par):
                dve.wait_ge(gathered[par][x], (t + (2 - par)) * (8 * SETS[x]))
                if x == 0:
                    dve.wait_ge(bd_ready, t)
                    dve.wait_ge(pairs_ready[1], t)
                src = emb[par][:, K * FIRST[x]:K * (FIRST[x] + SETS[x])]
                nc.vector.transpose(xe[:, XE0[x] * NS:(XE0[x] + SETS[x]) * NS], src).then_inc(xe_ready[x], 1)
                dve.wait_ge(xe_ready[x], t + 1)
                if x == 1:
                    for g in range(BD_BY_SCALAR, NG):
                        last = nc.vector.tensor_copy(bd_part(par, 1, g), xe_part(1, g))
                    last.then_inc(bd_by_vector, 1)
                w0 = XE0[x] + SETS[x]
                nc.vector.transpose(xe[:, w0 * NS:(w0 + WRAP[x]) * NS], src[:, 0:K * WRAP[x]]
                                    ).then_inc(wrapped[x], 1)
                dve.wait_ge(wrapped[x], t + 1)

            def within(col, n, f, d0, nd, m):
                return nc.vector.tensor_tensor(
                    view(pairs, col + d0 * n, [(NP, NS), (n, nd), (1, m)]),
                    view(xe, f * NS, [(1, NS), (0, nd), (NS, m)]),
                    view(xe, (f + d0) * NS, [(1, NS), (NS, nd), (NS, m)]), ALU.mult)

            def form_pairs(x, t, par, last=False):
                transpose_set(x, t, par)
                if x == 1 and not last:
                    copy_ids(t + 2, par)
                if not (isinstance(t, int) and t == 0):
                    dve.wait_ge(fills, fills_before(t) - NFILL + (x + 1) * FILLS)
                if x == 0:
                    nc.vector.tensor_copy(view(pairs, ONE_A, [(NP, NS), (1, NA)]),
                                          view(xe, XE0[0] * NS, [(1, NS), (NS, NA)]))
                n, col = SETS[x], (AA, WW)[x]
                within(col, n, XE0[x], n // 2, 1, n if n % 2 else n // 2)
                within(col, n, XE0[x], 0, n // 2, n).then_inc(pairs_ready[x], 1)

            def fold(dst_j, dst_col, dst_dims, src_j, src_col, src_dims):
                dst = view(v, dst_j * NV + dst_col, dst_dims)
                return nc.vector.tensor_tensor(dst, dst, view(v, src_j * NV + src_col, src_dims), ALU.add)

            def fold_shared(x, rnd):
                for k, a, da, b, db, m in kept_products(SETS[x], FIRST[x], (AA, WW)[x]):
                    if k == rnd:
                        last = nc.vector.tensor_tensor(view(v, b, [(db, m)]), view(v, b, [(db, m)]),
                                                       view(v, a, [(da, m)]), ALU.add)
                return last

            def fold_a():
                dve.wait_ge(emptied_s, emptied_by_scalar(V_FILL[NA - 1]))
                nc.vector.memset(linear[:], 0.0)
                fold_shared(0, 1).then_inc(v_folding, 1)
                dve.wait_ge(v_folding, 1)
                nc.vector.tensor_copy(linear[:, ONE_A:ONE_A + NA], view(v, ONE, [(NV, NA)]))
                fold_shared(0, 2).then_inc(v_folding, 1)

            def fold_v():
                dve.wait_ge(emptied_s, emptied_by_scalar(V_FILL[NF - 1]))
                fold_shared(1, 1).then_inc(v_folding, 1)
                dve.wait_ge(v_folding, FOLDED["W"] - 1)
                fold_shared(1, 2).then_inc(v_folding, 1)
                for half in range(2):
                    if half:
                        dve.wait_ge(v_folding, FOLDED["AA with w"] - 1)
                    for d, p, q, m in shifts(NA):
                        if half and d == 0:
                            continue
                        j, a = ((p, q), (q, p))[half]
                        last = fold(NA, AA + d * NA + p, [(NV, NW), (1, m)], j, AW + a, [(NA, NW), (NV + 1, m)])
                    last.then_inc(v_folding, 1)
                for half in range(2):
                    if half:
                        dve.wait_ge(v_folding, FOLDED["WW with a"] - 1)
                    for d, p, q, m in shifts(NW):
                        if half and d == 0:
                            continue
                        j, w = ((p, q), (q, p))[half]
                        last = fold(0, WW + d * NW + p, [(NV, NA), (1, m)],
                                    NA + j, AW + w * NA, [(1, NA), (NV + NA, m)])
                    last.then_inc(v_folding, 1)

            def empty_vt(n0, n1):
                for n in [f for f in BY_VECTOR if n0 <= f < n1]:
                    dve.wait_ge(fills, n + 1)
                    for dst, src in weight_parts(n):
                        last = nc.vector.tensor_copy(dst, src)
                    last.then_inc(emptied_v, 1)

            def split_dense_weights():
                dve.wait_ge(mlp_in, MLP_LOADS * 16)
                nc.vector.tensor_copy(wt1d[:], wt1d_sb[:]).then_inc(weights_hi, 1)
                dve.wait_ge(weights_hi, 1)
                for g in range(1, NG, 2):
                    part = wt1d[K * g:K * g + K, :]
                    last = nc.vector.tensor_tensor(part, wt1d_sb[K * g:K * g + K, :], part.bitcast(F32),
                                                   ALU.subtract)
                last.then_inc(dense_split, 1)

            form_pairs(0, 0, 0)
            fold_a()
            empty_vt(V_FILL0, PRE)
            form_pairs(1, 0, 0)
            fold_v()
            split_dense_weights()
            form_pairs(0, 1, 1)
            form_pairs(1, 1, 1)
            with dve.Fori(2, NT - 3, 2) as t:
                for u in range(2):
                    form_pairs(0, t + u, u)
                    form_pairs(1, t + u, u)
            for t in range(NT - 2, NT):
                form_pairs(0, t, t % 2)
                form_pairs(1, t, t % 2, last=True)

        @block.scalar
        def _(act):
            def copy(dst, src):
                return nc.scalar.activation(dst, src, ACT.Copy)

            def fill_block_diagonal(x, t, par, g0=0, g1=NG):
                act.wait_ge(xe_ready[x], t + 1)
                for g in range(g0, g1):
                    last = copy(bd_part(par, x, g), xe_part(x, g))
                if x == 1:
                    last.then_inc(bd_ready, 1)

            def empty_products(t, m0, m1):
                for m in range(m0, m1):
                    x = m // FILLS
                    act.wait_ge(fills, fills_before(t) + (m + 1))
                    bank = tile_bank(t, m)[:, 0:PER * NJ * NG].rearrange("r (u j g) -> r u j g", g=NG, j=NJ)
                    columns = slice(m % FILLS * PER, m % FILLS * PER + PER)
                    full = FIRST_SLOT[1 - x] - (1 - x)
                    copy(prod[0:ROWS[x], x, :, :].rearrange("r j (g s) -> r s j g", g=NG)[:, columns],
                         bank[0:ROWS[x], :, full:full + NA + 1, :])
                    for odd in range(2):
                        pairs_of = SHARED[x] - odd
                        own = FIRST_SLOT[x] + odd
                        last = copy(prod_shared[HALF * odd:HALF * odd + HALF, x, 0:pairs_of, :].rearrange(
                            "r j (g s) -> r s j g", g=NG)[:, columns],
                            bank[0:HALF, :, own:own + 2 * pairs_of - 1:2, :])
                    last.then_inc(emptied_s, 1)

            def empty_h1(t):
                act.wait_ge(h1_done, t + 1)
                for c in range(C1):
                    last = nc.scalar.activation(h1_sb[:, c, :], h1_ps[:, P * c:P * c + P], ACT.Relu,
                                                bias=bt1_sb[:, c:c + 1])
                last.then_inc(h1_ready, 1)

            def empty_h2(t):
                act.wait_ge(h2_done, t + 1)
                for c in range(C2):
                    last = nc.scalar.activation(h2_sb[:, c, :], h2_ps[:, P * c:P * c + P], ACT.Relu,
                                                bias=bt2_sb[:, c:c + 1])
                last.then_inc(h2_ready, 1)

            def empty_y(t):
                act.wait_ge(y_done, t + 1)
                copy(y_sb[:, bass.ds(t * P, P)], y_part).then_inc(y_ready, 1)

            def last_mlp():
                for c in range(C1):
                    act.wait_ge(last_h1_done, c + 1)
                    nc.scalar.activation(h1_sb[:, c, :], ring[c][:, 0:P], ACT.Relu,
                                         bias=bt1_sb[:, c:c + 1]).then_inc(last_h1_out, 1)
                act.wait_ge(h2_done, NT)
                for c in range(C2):
                    nc.scalar.activation(h2_sb[:, c, :], last_h2_ps[c][:, 0:P], ACT.Relu,
                                         bias=bt2_sb[:, c:c + 1]).then_inc(last_h2_out, 1)
                empty_y(NT - 1)

            def empty_z(t):
                act.wait_ge(z_done, t + 1)
                copy(z_sb[:, 0, :], z_ps[:, P:2 * P]).then_inc(z_ready, 1)
                nc.scalar.activation(z_sb[:, 1, :], z_ps[:, 0:P], ACT.Identity,
                                     bias=b2k[:, 0:1]).then_inc(z_ready, 1)

            def empty_vt(n0, n1):
                for n in range(n0, n1):
                    if n in BY_VECTOR:
                        continue
                    act.wait_ge(fills, n + 1)
                    for dst, src in weight_parts(n):
                        last = copy(dst, src)
                    last.then_inc(emptied_s, 1)

            def tile(t, par, first=False, last=False):
                empty_products(t, 0, FILLS)
                if not first:
                    empty_h1(t - 1)
                empty_products(t, FILLS, NFILL)
                if first:
                    empty_vt(ADDED_FILL0, TILE1)
                    act.wait_ge(ones_set, 2 * NG)
                else:
                    empty_h2(t - 1)
                if not last:
                    fill_block_diagonal(0, t + 1, 1 - par)
                if not first:
                    empty_y(t - 1)
                if not last:
                    fill_block_diagonal(1, t + 1, 1 - par, 0, BD_BY_SCALAR)
                empty_z(t)

            for n in range(DN_FILL0, DN_FILL0 + DN_FILLS):
                act.wait_ge(fills, n + 1)
                c = 4 * P * (n - DN_FILL0)
                copy(dense_t[:, c:c + 4 * P], ring_of(n)[:]).then_inc(dense_hi, 1)
            for n in [f for f in range(W2_FILL0, V_FILL0) if f not in BY_VECTOR]:
                act.wait_ge(fills, n + 1)
                copy(w2t_of(n), ring_of(n)[:, 0:w2_fields(n) * P]).then_inc(emptied_s, 1)
            act.wait_ge(ones_set, NG)
            for j in range(NF):
                act.wait_ge(fills, V_FILL[j] + 1)
                copy(v[:, j * NV:j * NV + NV], ring_of(V_FILL[j])[:, 0:NV]).then_inc(emptied_s, 1)
                if vt_run(V_FILL[j] + 1) in VT_OF_W1:
                    empty_vt(V_FILL[j] + 1, V_FILL[j] + 2)
                if 0 <= j - (NF - 11) < NG:
                    fill_block_diagonal(0, 0, 0, j - (NF - 11), j - (NF - 11) + 1)
            act.wait_ge(mlp_in, MLP_LOADS * 16)
            nc.scalar.mul(b2k[:], b2_sb[:], float(K)).then_inc(b2_scaled, 1)
            fill_block_diagonal(1, 0, 0, 0, BD_BY_SCALAR)
            empty_vt(PRE - len(VT_OF_A), PRE)
            act.wait_ge(b2_scaled, 1)
            tile(0, 0, first=True)
            with act.Fori(1, NT - 1, 2) as t:
                for u in range(2):
                    tile(t + u, 1 - u)
            tile(NT - 1, 1, last=True)
            last_mlp()

        @block.tensor
        def _(pe):
            def early_slot(n):
                if n >= RING:
                    if n - RING in BY_VECTOR:
                        pe.wait_ge(emptied_v, emptied_by_vector(n - RING))
                    else:
                        pe.wait_ge(emptied_s, emptied_by_scalar(n - RING))

            def products(t, par, m0, m1):
                for m in range(m0, m1):
                    x = m // FILLS
                    if m % FILLS == 0:
                        pe.wait_ge(pairs_ready[x], t + 1)
                        pe.wait_ge(bd_ready, t + 1)
                        pe.wait_ge(bd_by_vector, t + 1)
                    if isinstance(t, int) and t == 0:
                        early_slot(PRE + m)
                    else:
                        pe.wait_ge(emptied_s, emptied_s_at(t, m - RING))
                    for u in range(PER):
                        s = m % FILLS * PER + u
                        mm = pe.matmul(tile_bank(t, m)[0:ROWS[x], u * NJ * NG:(u + 1) * NJ * NG],
                                       pairs[:, s, ROW0[x]:ROW0[x] + ROWS[x]],
                                       bd[par][:, s].rearrange("p j g -> p (j g)"), start=True, stop=True)
                    mm.then_inc(fills, 1)

            def interactions(t, x):
                pe.wait_ge(emptied_s, emptied_s_at(t, (x + 1) * FILLS - 1))
                for f in range(NA):
                    slot = f + (1 - x)
                    pe.matmul(z_ps[:, 0:P], vt[0:ROWS[x], VT0[x] + slot, :], prod[0:ROWS[x], x, slot, :],
                              start=(x, f) == (0, 0), stop=False)
                if x == 0:
                    pe.matmul(z_ps[:, 0:P], vt[0:ROWS[0], VT_LINEAR, :], prod[0:ROWS[0], 0, 0, :],
                              start=False, stop=False)
                for m in range(SHARED[x]):
                    b = VT_SHARED[x] + m
                    pe.matmul(z_ps[:, 0:P], vt[0:block_rows(b), b, :], prod_shared[0:block_rows(b), x, m, :],
                              start=False, stop=(x, m) == (1, SHARED[1] - 1))

            def first_order(t):
                for x in range(2):
                    pe.matmul(z_ps[:, P:2 * P], vt[0:ROWS[x], VT_ONE[x], :], prod[0:ROWS[x], x, NA * x, :],
                              start=x == 0, stop=False)
                pe.wait_ge(cross_in, (t + 1) * (16 * NW))
                for c in range(2):
                    mm = pe.matmul(z_ps[:, P:2 * P], vt[0:CROSS[c], VT_CROSS + c, :], cross_sb[0:CROSS[c], c, :],
                                   start=False, stop=c == 1)
                mm.then_inc(z_done, 1)

            def layer1_of_z(dst, c, k, start=False, stop=False):
                return pe.matmul(dst, wt1_sb[:, k, P * c:P * c + P], z_sb[:, k, :], start=start, stop=stop)

            def layer1_of_dense(dst, c, t, start=False, stop=False):
                return pe.matmul(dst, wt1d[:, P * c:P * c + P], dense_t[:, bass.ds(t * P, P)],
                                 start=start, stop=stop)

            def layer1(t):
                pe.wait_ge(z_ready, t * 2 + 2)
                for c in range(C1):
                    dst = h1_ps[:, P * c:P * c + P]
                    layer1_of_z(dst, c, 0, start=True)
                    layer1_of_z(dst, c, 1)
                    mm = layer1_of_dense(dst, c, t, stop=True)
                mm.then_inc(h1_done, 1)

            def layer2(t):
                pe.wait_ge(h1_ready, t + 1)
                for c in range(C2):
                    for k in range(C1):
                        mm = pe.matmul(h2_ps[:, P * c:P * c + P], wt2_sb[:, k, P * c:P * c + P],
                                       h1_sb[:, k, :], start=k == 0, stop=k == C1 - 1)
                mm.then_inc(h2_done, 1)

            def layer3(t):
                pe.wait_ge(h2_ready, t + 1)
                for k in range(C2):
                    mm = pe.matmul(y_part, wt3_sb[:, k:k + 1], h2_sb[:, k, :], start=k == 0, stop=k == C2 - 1)
                mm.then_inc(y_done, 1)

            def last_mlp():
                for c in range(C1):
                    layer1_of_dense(ring[c][:, 0:P], c, NT - 1, start=True)
                pe.wait_ge(z_ready, 2 * NT - 1)
                for c in range(C1):
                    layer1_of_z(ring[c][:, 0:P], c, 0)
                pe.wait_ge(z_ready, 2 * NT)
                for c in range(C1):
                    layer1_of_z(ring[c][:, 0:P], c, 1, stop=True).then_inc(last_h1_done, 1)
                for k in range(C1):
                    pe.wait_ge(last_h1_out, k + 1)
                    for c in range(C2):
                        mm = pe.matmul(last_h2_ps[c][:, 0:P], wt2_sb[:, k, P * c:P * c + P], h1_sb[:, k, :],
                                       start=k == 0, stop=k == C1 - 1)
                mm.then_inc(h2_done, 1)
                for k in range(C2):
                    pe.wait_ge(last_h2_out, k + 1)
                    mm = pe.matmul(y_part, wt3_sb[:, k:k + 1], h2_sb[:, k, :], start=k == 0, stop=k == C2 - 1)
                mm.then_inc(y_done, 1)

            def turn_v(n0, n1):
                for n in range(n0, n1):
                    b0, m = vt_run(n)
                    early_slot(n)
                    for b in range(b0, b0 + m):
                        rows = block_rows(b)
                        at = P * (b - b0)
                        if b in VT_ONE:
                            x = VT_ONE.index(b)
                            sources = [w1s[:, ROW0[x]:ROW0[x] + rows]]
                        elif b < VT_SHARED[0]:
                            x = int(b > NW)
                            c = (b - VT0[x] + (NA - 1) * (1 - x)) * NV + ROW0[x]
                            sources = [v[:, c:c + rows]]
                        elif b < VT_CROSS:
                            x = int(b >= VT_SHARED[1])
                            c = (FIRST[x] + 2 * (b - VT_SHARED[x])) * NV + (AA, WW)[x]
                            sources = [v[:, c + NV * i:c + NV * i + HALF] for i in range(rows // HALF)]
                            at, rows = 2 * at, HALF
                        elif b < VT_LINEAR:
                            c = AW + (b - VT_CROSS) * CROSS[0]
                            sources = [w1s[:, c:c + rows]]
                        else:
                            sources = [linear[:]]
                        for i, src in enumerate(sources):
                            mm = pe.transpose(ring_of(n)[0:rows, at + P * i:at + P * i + P], src, ident[:])
                    mm.then_inc(fills, 1)

            def tile(t, par, first=False):
                products(t, par, 0, FILLS)
                if not first:
                    layer1(t - 1)
                products(t, par, FILLS, NFILL)
                if first:
                    n = ADDED_FILL0
                    for runs, what in ((VT_OF_W, "W"), (VT_AA_W, "AA with w"), (VT_WW_A, "WW with a")):
                        pe.wait_ge(v_folding, FOLDED[what])
                        turn_v(n, n + len(runs))
                        n += len(runs)
                    pe.wait_ge(emptied_v, emptied_by_vector(TILE1 - 1))
                    pe.wait_ge(emptied_s, emptied_by_scalar(TILE1 - 1))
                    pe.wait_ge(mlp_in, MLP_LOADS * 16)
                    pe.wait_ge(dense_split, 1)
                if not first:
                    layer2(t - 1)
                interactions(t, 0)
                if not first:
                    layer3(t - 1)
                interactions(t, 1)
                first_order(t)

            pe.wait_ge(ident_ready, 1)
            pe.wait_ge(dense_spread, 1)
            for n in range(DN_FILLS):
                for u in range(4):
                    mm = pe.transpose(ring_of(DN_FILL0 + n)[:, P * u:P * u + P], dense4[:, 4 * n + u, :], ident[:])
                mm.then_inc(fills, 1)
            pe.wait_ge(w2_in, 16)
            for n in range(W2_FILL0, V_FILL0):
                early_slot(n)
                for u in range(w2_fields(n)):
                    mm = pe.transpose(ring_of(n)[:, P * u:P * u + P], w2_sb[:, :, 4 * (n - W2_FILL0) + u], ident[:])
                mm.then_inc(fills, 1)
            pe.wait_ge(w1_folded, 1)
            for n in range(V_FILL0, PRE):
                if vt_run(n):
                    if vt_run(n) in VT_OF_A:
                        pe.wait_ge(v_folding, FOLDED["A"])
                    turn_v(n, n + 1)
                else:
                    early_slot(n)
                    if EARLY[n - V_FILL0] % 4 == 0:
                        of = W2_FILL0 + EARLY[n - V_FILL0] // 4
                        if of in BY_VECTOR:
                            pe.wait_ge(emptied_v, emptied_by_vector(of))
                        else:
                            pe.wait_ge(emptied_s, emptied_by_scalar(of))
                    pe.matmul(ring_of(n)[:, 0:NV], w2t[:, EARLY[n - V_FILL0], :], w1s[:],
                              start=True, stop=True).then_inc(fills, 1)
            tile(0, 0, first=True)
            with pe.Fori(1, NT - 1, 2) as t:
                for u in range(2):
                    tile(t + u, 1 - u)
            tile(NT - 1, 1)
            last_mlp()


def kernel(**inputs):
    import numpy as np
    import concourse.bacc as bacc
    from concourse.bass_utils import run_bass_kernel_spmd

    nc = bacc.Bacc("TRN2", target_bir_lowering=False, num_devices=1)
    arrays = {}

    def dram(name):
        a = np.ascontiguousarray(inputs[name])
        arrays[f"in_{name}"] = a
        return nc.dram_tensor(f"in_{name}", a.shape, mybir.dt.from_np(a.dtype), kind="ExternalInput").ap()

    tables = [dram(f"tbl_{f}") for f in range(26)]
    dense, ids = dram("dense_ctx"), dram("ids")
    mlp = [dram(n) for n in ("W_top1", "b_top1", "W_top2", "b_top2", "W_top3")]
    cin = [dram(n) for n in ("L0_rec_W1", "L0_rec_b1", "L0_rec_W2", "L0_rec_b2")]
    out = nc.dram_tensor("out_y", (dense.shape[0], 1), F32, kind="ExternalOutput").ap()
    dlrm_kernel(nc, dense, ids, tables, *mlp, *cin, out)
    r = run_bass_kernel_spmd(nc, [arrays], core_ids=[0])
    return r.results[0]["out_y"]
```
